# Optimizing a Trainium2 kernel written in Bass

```python
import numpy as np
import jax
import jax.numpy as jnp

def _softmax(x, axis=-1):
    return jax.nn.softmax(x, axis=axis)

def _gelu(x):
    return jax.nn.gelu(x, approximate=True)

def _silu(x):
    return jax.nn.silu(x)

def _sigmoid(x):
    return jax.nn.sigmoid(x)

def _layernorm(x, axis=-1, eps=1e-05):
    m = jnp.mean(x, axis=axis, keepdims=True)
    v = jnp.var(x, axis=axis, keepdims=True)
    return (x - m) / jnp.sqrt(v + eps)

def _scatter_add(tgt, idx, src, axis=0):
    return tgt.at[idx].add(src)

def _segment_sum(src, seg, n):
    return jax.ops.segment_sum(src, seg, n)
kernel_name = 'mk_adaln_d1_jaxref_r8_e18a4b'

def setup_inputs(seed: int=0):
    np.random.seed(seed)
    _w = jnp.asarray

    def _L0_attn_setup():
        import jax, jax.numpy as jnp
        import numpy as np
        B, L, HID = (2, 512, 256)
        H, D = (16, HID // 16)
        C = 64
        LOWR = 16
        GLN = 16.0
        EPS = 1e-05

        def _gla_forward(x, Wq, Wk, Wv, Wg1, Wg2, bg2, Wgate, norm_w, Wo):
            Bx, Lx, _ = x.shape
            NC = Lx // C
            scale = D ** (-0.5)

            def heads(y):
                return y.reshape(Bx, Lx, H, D).transpose(0, 2, 1, 3)
            q = heads(x @ Wq)
            k = heads(x @ Wk)
            v = heads(x @ Wv)
            gk = heads(jax.nn.log_sigmoid(x @ Wg1 @ Wg2 + bg2) / GLN)

            def chunked(y):
                return y.reshape(Bx, H, NC, C, D).transpose(2, 0, 1, 3, 4)
            qc, kc, vc = (chunked(q), chunked(k), chunked(v))
            Gc = jnp.cumsum(chunked(gk), axis=3)
            tril = jnp.tril(jnp.ones((C, C), bool))
            S0 = jnp.zeros((Bx, H, D, D), jnp.float32)

            def step(S, inp):
                Q, K, V, G = inp
                Gbase = G[:, :, 0]
                qg = Q * scale * jnp.exp(G)
                o_inter = jnp.einsum('bhld,bhdv->bhlv', qg, S)
                Qh = Q * jnp.exp(G - Gbase[:, :, None]) * scale
                Kh = K * jnp.exp(Gbase[:, :, None] - G)
                A = jnp.einsum('bhld,bhsd->bhls', Qh, Kh)
                A = jnp.where(tril, A, 0.0)
                o_intra = jnp.einsum('bhls,bhsv->bhlv', A, V)
                glast = G[:, :, -1]
                Ks = K * jnp.exp(glast[:, :, None] - G)
                S_new = S * jnp.exp(glast)[..., None] + jnp.einsum('bhld,bhlv->bhdv', Ks, V)
                return (S_new, o_inter + o_intra)
            S_final, o_chunks = jax.lax.scan(step, S0, (qc, kc, vc, Gc))
            o = o_chunks.transpose(1, 3, 0, 2, 4).reshape(Bx, Lx, H, D)
            o = o_chunks.transpose(1, 2, 0, 3, 4).reshape(Bx, H, Lx, D).transpose(0, 2, 1, 3)
            o = o * jax.lax.rsqrt(jnp.mean(o * o, axis=-1, keepdims=True) + EPS) * norm_w
            o = o.reshape(Bx, Lx, HID)
            g = x @ Wgate
            o = o * (g * jax.nn.sigmoid(g))
            return (o @ Wo, S_final)

        def _reference_tuple_inner(x, Wq, Wk, Wv, Wg1, Wg2, bg2, Wgate, norm_w, Wo):
            return _gla_forward(x, Wq, Wk, Wv, Wg1, Wg2, bg2, Wgate, norm_w, Wo)
        key = jax.random.key(seed)
        ks = jax.random.split(key, 10)
        s = lambda fan_in: 1.0 / np.sqrt(fan_in)
        return {'x': jax.random.normal(ks[0], (B, L, HID), jnp.float32), 'Wq': jax.random.normal(ks[1], (HID, HID), jnp.float32) * s(HID), 'Wk': jax.random.normal(ks[2], (HID, HID), jnp.float32) * s(HID), 'Wv': jax.random.normal(ks[3], (HID, HID), jnp.float32) * s(HID), 'Wg1': jax.random.normal(ks[4], (HID, LOWR), jnp.float32) * s(HID), 'Wg2': jax.random.normal(ks[5], (LOWR, HID), jnp.float32) * s(LOWR), 'bg2': jax.random.normal(ks[6], (HID,), jnp.float32) * 0.1, 'Wgate': jax.random.normal(ks[7], (HID, HID), jnp.float32) * s(HID), 'norm_w': jnp.ones((D,), jnp.float32), 'Wo': jax.random.normal(ks[8], (HID, HID), jnp.float32) * s(HID)}
    _L0_attn_in = _L0_attn_setup()

    def _L0_ffn_setup():
        import jax, jax.numpy as jnp
        import numpy as np
        B, T, C = (2, 128, 256)
        E, TOPK = (8, 2)
        F_MOE = 176
        F_SHARED = 704
        key = jax.random.key(seed)
        ks = jax.random.split(key, 9)
        s = 0.02
        return {'x': jax.random.normal(ks[0], (B, T, C), dtype=jnp.float32), 'gate_w': jax.random.normal(ks[1], (E, C), dtype=jnp.float32) * s, 'expert_fc1': jax.random.normal(ks[2], (E, F_MOE, C), dtype=jnp.float32) * s, 'expert_fc2': jax.random.normal(ks[3], (E, F_MOE, C), dtype=jnp.float32) * s, 'expert_proj': jax.random.normal(ks[4], (E, C, F_MOE), dtype=jnp.float32) * s, 'shared_fc1': jax.random.normal(ks[5], (F_SHARED, C), dtype=jnp.float32) * s, 'shared_fc2': jax.random.normal(ks[6], (F_SHARED, C), dtype=jnp.float32) * s, 'shared_proj': jax.random.normal(ks[7], (C, F_SHARED), dtype=jnp.float32) * s, 'shared_gate_w': jax.random.normal(ks[8], (1, C), dtype=jnp.float32) * s}
    _L0_ffn_in = _L0_ffn_setup()
    _L0_c = _w((lambda *s: np.random.randn(*s).astype(np.float32) * 0.05)(2, 256))
    _L0_wmod = _w((lambda *s: np.random.randn(*s).astype(np.float32) * 0.05)(256, 6 * 256) * 256 ** (-0.5))
    _d = {'L0_attn_x': _L0_attn_in['x'], 'L0_attn_Wq': _L0_attn_in['Wq'], 'L0_attn_Wk': _L0_attn_in['Wk'], 'L0_attn_Wv': _L0_attn_in['Wv'], 'L0_attn_Wg1': _L0_attn_in['Wg1'], 'L0_attn_Wg2': _L0_attn_in['Wg2'], 'L0_attn_bg2': _L0_attn_in['bg2'], 'L0_attn_Wgate': _L0_attn_in['Wgate'], 'L0_attn_norm_w': _L0_attn_in['norm_w'], 'L0_attn_Wo': _L0_attn_in['Wo'], 'L0_ffn_gate_w': _L0_ffn_in['gate_w'], 'L0_ffn_expert_fc1': _L0_ffn_in['expert_fc1'], 'L0_ffn_expert_fc2': _L0_ffn_in['expert_fc2'], 'L0_ffn_expert_proj': _L0_ffn_in['expert_proj'], 'L0_ffn_shared_fc1': _L0_ffn_in['shared_fc1'], 'L0_ffn_shared_fc2': _L0_ffn_in['shared_fc2'], 'L0_ffn_shared_proj': _L0_ffn_in['shared_proj'], 'L0_ffn_shared_gate_w': _L0_ffn_in['shared_gate_w'], 'L0_c': _L0_c, 'L0_wmod': _L0_wmod}
    _x0 = _d['L0_attn_x']
    _d['L0_attn_x'] = jax.random.normal(jax.random.fold_in(jax.random.key(seed), 1), (2, 1024, 256), dtype=_x0.dtype)
    del _x0
    return _d

def reference(L0_attn_x, L0_attn_Wq, L0_attn_Wk, L0_attn_Wv, L0_attn_Wg1, L0_attn_Wg2, L0_attn_bg2, L0_attn_Wgate, L0_attn_norm_w, L0_attn_Wo, L0_ffn_gate_w, L0_ffn_expert_fc1, L0_ffn_expert_fc2, L0_ffn_expert_proj, L0_ffn_shared_fc1, L0_ffn_shared_fc2, L0_ffn_shared_proj, L0_ffn_shared_gate_w, L0_c, L0_wmod):

    def _L0_attn_ref(x, Wq, Wk, Wv, Wg1, Wg2, bg2, Wgate, norm_w, Wo):
        import jax, jax.numpy as jnp
        import numpy as np
        B, L, HID = (2, 512, 256)
        H, D = (16, HID // 16)
        C = 64
        LOWR = 16
        GLN = 16.0
        EPS = 1e-05

        def _gla_forward(x, Wq, Wk, Wv, Wg1, Wg2, bg2, Wgate, norm_w, Wo):
            Bx, Lx, _ = x.shape
            NC = Lx // C
            scale = D ** (-0.5)

            def heads(y):
                return y.reshape(Bx, Lx, H, D).transpose(0, 2, 1, 3)
            q = heads(x @ Wq)
            k = heads(x @ Wk)
            v = heads(x @ Wv)
            gk = heads(jax.nn.log_sigmoid(x @ Wg1 @ Wg2 + bg2) / GLN)

            def chunked(y):
                return y.reshape(Bx, H, NC, C, D).transpose(2, 0, 1, 3, 4)
            qc, kc, vc = (chunked(q), chunked(k), chunked(v))
            Gc = jnp.cumsum(chunked(gk), axis=3)
            tril = jnp.tril(jnp.ones((C, C), bool))
            S0 = jnp.zeros((Bx, H, D, D), jnp.float32)

            def step(S, inp):
                Q, K, V, G = inp
                Gbase = G[:, :, 0]
                qg = Q * scale * jnp.exp(G)
                o_inter = jnp.einsum('bhld,bhdv->bhlv', qg, S)
                Qh = Q * jnp.exp(G - Gbase[:, :, None]) * scale
                Kh = K * jnp.exp(Gbase[:, :, None] - G)
                A = jnp.einsum('bhld,bhsd->bhls', Qh, Kh)
                A = jnp.where(tril, A, 0.0)
                o_intra = jnp.einsum('bhls,bhsv->bhlv', A, V)
                glast = G[:, :, -1]
                Ks = K * jnp.exp(glast[:, :, None] - G)
                S_new = S * jnp.exp(glast)[..., None] + jnp.einsum('bhld,bhlv->bhdv', Ks, V)
                return (S_new, o_inter + o_intra)
            S_final, o_chunks = jax.lax.scan(step, S0, (qc, kc, vc, Gc))
            o = o_chunks.transpose(1, 3, 0, 2, 4).reshape(Bx, Lx, H, D)
            o = o_chunks.transpose(1, 2, 0, 3, 4).reshape(Bx, H, Lx, D).transpose(0, 2, 1, 3)
            o = o * jax.lax.rsqrt(jnp.mean(o * o, axis=-1, keepdims=True) + EPS) * norm_w
            o = o.reshape(Bx, Lx, HID)
            g = x @ Wgate
            o = o * (g * jax.nn.sigmoid(g))
            return (o @ Wo, S_final)

        def _reference_tuple_inner(x, Wq, Wk, Wv, Wg1, Wg2, bg2, Wgate, norm_w, Wo):
            return _gla_forward(x, Wq, Wk, Wv, Wg1, Wg2, bg2, Wgate, norm_w, Wo)
        return _reference_tuple_inner(x, Wq, Wk, Wv, Wg1, Wg2, bg2, Wgate, norm_w, Wo)[0]

    def _L0_ffn_ref(x, gate_w, expert_fc1, expert_fc2, expert_proj, shared_fc1, shared_fc2, shared_proj, shared_gate_w):
        import jax, jax.numpy as jnp
        import numpy as np
        B, T, C = (2, 128, 256)
        E, TOPK = (8, 2)
        F_MOE = 176
        F_SHARED = 704
        b, t, c = x.shape
        xf = x.reshape(-1, c)
        n = xf.shape[0]
        router = xf @ gate_w.T
        probs = jax.nn.softmax(router.astype(jnp.float32), axis=1).astype(x.dtype)
        top_p, top_i = jax.lax.top_k(probs, TOPK)
        combine = jnp.zeros((n, E), dtype=x.dtype).at[jnp.arange(n)[:, None], top_i].set(top_p)
        h1 = jnp.einsum('nc,efc->enf', xf, expert_fc1)
        h2 = jnp.einsum('nc,efc->enf', xf, expert_fc2)
        h = jax.nn.silu(h1) * h2
        out_e = jnp.einsum('enf,ecf->enc', h, expert_proj)
        y = jnp.einsum('ne,enc->nc', combine, out_e)
        s1 = xf @ shared_fc1.T
        s2 = xf @ shared_fc2.T
        shared = jax.nn.silu(s1) * s2 @ shared_proj.T
        y = y + jax.nn.sigmoid(xf @ shared_gate_w.T) * shared
        return y.reshape(b, t, c)
    x = L0_attn_x
    mod = (_silu(L0_c) @ L0_wmod).reshape(L0_c.shape[0], 6, 1, -1)
    sa, ca, ga, sb, cb, gb = (mod[:, 0], mod[:, 1], mod[:, 2], mod[:, 3], mod[:, 4], mod[:, 5])
    ga = (2 * (ga >= 0) - 1) * jnp.maximum(jnp.abs(ga), 0.25)
    gb = (2 * (gb >= 0) - 1) * jnp.maximum(jnp.abs(gb), 0.25)
    h = _layernorm(x, axis=-1) * (1 + ca) + sa
    x = x + ga * _L0_attn_ref(h, L0_attn_Wq, L0_attn_Wk, L0_attn_Wv, L0_attn_Wg1, L0_attn_Wg2, L0_attn_bg2, L0_attn_Wgate, L0_attn_norm_w, L0_attn_Wo)
    h = _layernorm(x, axis=-1) * (1 + cb) + sb
    x = x + gb * _L0_ffn_ref(h, L0_ffn_gate_w, L0_ffn_expert_fc1, L0_ffn_expert_fc2, L0_ffn_expert_proj, L0_ffn_shared_fc1, L0_ffn_shared_fc2, L0_ffn_shared_proj, L0_ffn_shared_gate_w)
    return x

_drawn_inputs = setup_inputs


def setup_inputs(seed=0):
    import zlib

    import numpy as np

    out = dict(_drawn_inputs(seed))
    spreads = {'L0_attn_norm_w': (1.0, 0.2)}
    factors = {'L0_attn_Wg1': 3.544,
     'L0_attn_Wg2': 3.31,
     'L0_attn_bg2': 7.201,
     'L0_ffn_gate_w': 8.0,
     'L0_ffn_expert_fc1': 8.0,
     'L0_ffn_expert_fc2': 8.0,
     'L0_ffn_expert_proj': 8.0,
     'L0_ffn_shared_fc1': 8.0,
     'L0_ffn_shared_fc2': 8.0,
     'L0_ffn_shared_proj': 8.0,
     'L0_ffn_shared_gate_w': 8.0}
    for name, (base, spread) in spreads.items():
        noise = np.random.default_rng([zlib.crc32(name.encode()), seed]).standard_normal(out[name].shape)
        drawn = base * np.exp(spread * noise) if base else spread * noise
        out[name] = jnp.asarray(drawn.astype(out[name].dtype))
    for name, factor in factors.items():
        out[name] = (out[name] * factor).astype(out[name].dtype)
    return out
```

```python
from contextlib import ExitStack

import concourse.bass as bass
from concourse import mybir

F32 = mybir.dt.float32
U32 = mybir.dt.uint32
I32 = mybir.dt.int32
ALU = mybir.AluOpType
ACT = mybir.ActivationFunctionType
AX_X = mybir.AxisListType.X

P = 128
BATCH, SEQ, HID = 2, 1024, 256
HEADS, HEAD = 16, 16
CHUNK = 64
LOWR = 16
GATE_NORM = 16.0
EPS = 1e-5
NE, TOPK, FE, FS = 8, 2, 176, 704
TOK = BATCH * SEQ
KC = HID // P
NTILE = TOK // P
BLK = 512
NBLK = TOK // BLK
BPB = SEQ // BLK
TPB = BLK // P
CPB = BLK // CHUNK
NPAIR = P // 32
FEH = FE // 2
FTS = (FS + P - 1) // P
ETILES = 40
EGRP = 4
XS_ROWS = ETILES * P
NROUT = NE + 1
SCALE = HEAD ** -0.5
SH_F = [(f * P, min(P, FS - f * P)) for f in range(FTS)]

def unit_order():
    units = [("MODC", 0, 0)] + [("MODR", b, h) for b in range(BATCH) for h in range(2)]

    def both(kind, blk):
        units.extend([(kind, blk, 0), (kind, blk, 1)])

    def shared_up(blk):
        for f in range(FTS):
            units.extend([("SA", blk, f), ("SB", blk, f)])

    for s in range(NBLK + 1):
        now, before = s < NBLK, s >= 1
        if now:
            both("XT", s)
            units.append(("LR", s, 0))
            both("Z", s)
            both("G", s)
            both("V", s)
        if before:
            both("MS", s - 1)
        if now:
            both("K", s)
        if before:
            both("WO", s - 1)
        if now:
            both("Q", s)
            both("KT", s)
            both("KV", s)
        if before:
            both("HT", s - 1)
            units.append(("RT", s - 1, 0))
        for blk in SHARED_AFTER.get(s, ()):
            shared_up(blk)
            if blk == RANK_IN:
                units.append(("RK", 0, 0))
            both("SD", blk)
    shared_up(NBLK - 1)
    both("SD", NBLK - 1)
    return units


SHARED_AFTER = {1: (0,), 3: (1,), 4: (2,)}
RANK_IN = 2
UNITS = unit_order()
TURN = {key: n for n, key in enumerate(UNITS)}


def free_dims(ap, dims):
    return bass.AP(ap.tensor, ap.offset, [list(ap.ap[0])] + [list(d) for d in dims])


def adaln_moe(nc, x, cT, wmod, wq, wk, wv, wg1, wg2, bg2, wgate, norm_w, wo,
              router, e_up, e_down, s_up, s_down, out):
    with ExitStack() as ctx:
        def sb(name, shape, dt=F32):
            return ctx.enter_context(nc.sbuf_tensor(name, shape, dt))

        def ps(name, shape):
            return ctx.enter_context(nc.psum_tensor(name, shape, F32))

        def sem(name):
            return ctx.enter_context(nc.semaphore(name))

        xs_dram = nc.dram_tensor("xs_sorted", (XS_ROWS, HID), F32, kind="Internal").ap()
        ys_dram = nc.dram_tensor("ys_sorted", (XS_ROWS, HID), F32, kind="Internal").ap()

        work = [ps("work0", [P, 512]), ps("work1", [P, 512])]
        at_ps = [ps(f"at_ps{j}", [P, 512]) for j in range(NPAIR)]
        o_ps = [ps("o_even", [P, 512]), ps("o_odd", [P, 512])]

        x_sb = sb("x_sb", [P, NTILE, HID])
        xn = sb("xn", [P, TPB, HID])
        xn2 = sb("xn2", [P, TPB, HID])
        h2tok = sb("h2tok", [P, NTILE, HID])
        h2T = sb("h2T", [P, 2, KC, BLK])
        hT = sb("hT", [P, KC, BLK])
        tT = sb("tT", [33, BLK])
        za = sb("za", [P, KC, BLK])
        ktok = za[:, :, :].rearrange("p g (t c) -> p t g c", t=TPB)
        gk = sb("gk", [P, KC, BLK])
        er_pos = sb("er_pos", [P, KC, BLK])
        er_neg = sb("er_neg", [P, KC, BLK])
        arena = sb("arena", [P, 12288])
        taken = [0]

        def part(n):
            taken[0] += n
            assert taken[0] <= 12288
            return arena[:, taken[0] - n:taken[0]]

        qeo = part(KC * BLK * 2).rearrange("p (g c h l) -> p g c h l", g=KC, c=CPB, h=2)
        kh = part(KC * BLK).rearrange("p (g n) -> p g n", g=KC)
        qf = part(KC * BLK).rearrange("p (g n) -> p g n", g=KC)
        vpad = part(TPB * KC * NPAIR * 64).rearrange("p (t r w) -> p t r w", t=TPB, r=KC * NPAIR)
        tbd = part(KC * CPB * P).rearrange("p (g c n) -> p g c n", g=KC, c=CPB)
        atm = part(2 * NPAIR * 512).rearrange("p (a j n) -> p a j n", a=2, j=NPAIR)
        wmod_sb = arena[:, 0:KC * 6 * HID].rearrange("p (k n) -> p k n", k=KC)
        atm_zero = atm[:, 0, 0:2, :].rearrange("p j (t c) -> p (j t) c", c=HID)
        taken[0] = 0
        eup = part(NE * KC * 2 * FE).rearrange("p (e k n) -> p e k n", e=NE, k=KC)
        edn = part(NE * 2 * HID).rearrange("p (e k n) -> p e k n", e=NE, k=2)
        xt = part(2 * 2 * HID).rearrange("p (a t c) -> p a t c", a=2, t=2)
        xT = part(2 * KC * P).rearrange("p (a n) -> p a n", a=2)
        esil = part(2 * FE).rearrange("p (a n) -> p a n", a=2)
        hTe = part(2 * 2 * P).rearrange("p (a n) -> p a n", a=2)
        gbase = sb("gbase", [P, KC, CPB])
        f_base = sb("f_base", [P, KC, CPB])
        f_last = sb("f_last", [P, KC, CPB])
        f_all = sb("f_all", [P, KC, CPB])
        decay = sb("decay", [P, KC, 32, CPB])
        kv_in = sb("kv_in", [P, KC, 32, CPB])
        state = sb("state", [P, 2, KC, 32, CPB])
        carry = sb("carry", [P, KC, 32])
        tmask = sb("tmask", [P, KC, CPB, 32])
        sq = sb("sq", [P, 2, 512])
        yT = sb("yT", [P, KC, BLK])
        sg = sb("sg", [P, 2, KC, BLK])
        tmp = sb("tmp", [P, 2, HID])
        hs = sb("hs", [P, FTS, BLK])

        rows = sb("rows", [P, BATCH, 4, HID])
        GA, SB_, CB1, GB = range(4)
        cols = sb("cols", [P, 2, KC, BATCH])
        csb = sb("csb", [P, KC, BATCH])
        csil = sb("csil", [P, KC, BATCH])

        sgn, mag = (qf[:, b, :].rearrange("p (b c) -> p b c", b=BATCH) for b in range(2))
        csil_b = sg[:, 0, 0, :].rearrange("p (k b n) -> p k b n", k=KC, b=BATCH)
        yflat = yT[:, :, :].rearrange("p k n -> p (k n)")
        onehot = yflat[:, 0:256].rearrange("p (k t e) -> p k t e", k=TOPK, t=NTILE)
        picked, dlog, posf = (yflat[:, i:i + P].rearrange("p (t e) -> p t e", t=NTILE) for i in (256, 384, 512))
        tot, incl, base = (yflat[:, i:i + P].rearrange("p (e t) -> p e t", e=NE) for i in (640, 768, 896))
        tge = sg[:, 1, 0, 0:ETILES * NE].rearrange("p (i e) -> p i e", e=NE)
        pprod = sg[:, 1, 1, 0:P].rearrange("p (t e) -> p t e", t=NTILE)

        wq_sb, wk_sb, wv_sb, wgate_sb, wo_sb = (sb(n, [P, KC, HID]) for n in
                                                ("wq_sb", "wk_sb", "wv_sb", "wgate_sb", "wo_sb"))
        wg1_sb = sb("wg1_sb", [P, KC, LOWR])
        wg2_sb = sb("wg2_sb", [33, HID])
        nw_sb = sb("nw_sb", [P, 1])
        rout_sb = sb("rout_sb", [P, KC, NROUT])
        sup_sb = sb("sup_sb", [P, KC, 2, FS])
        sdn_sb = sb("sdn_sb", [P, FTS, HID])

        ident = sb("ident", [P, P])
        tri = sb("tri", [P, P])
        ones = sb("ones", [P, P])
        bd16 = sb("bd16", [P, P])
        pmask = sb("pmask", [P, 32])
        qsel = sb("qsel", [P, 2])
        causal = sb("causal", [P, 2 * NPAIR, CHUNK])
        eps_c = sb("eps_c", [P, 1])
        iota_i = sb("iota_i", [P, ETILES], I32)
        iota_f = sb("iota_f", [P, ETILES])

        stats = sb("stats", [P, 2, TPB, 6])
        mv = sb("mv", [P, 2, TPB, 2])
        lnv = sb("lnv", [P, 2, TPB])
        rstd = sb("rstd", [P, 2, TPB])
        nmr = sb("nmr", [P, 2, TPB])
        logits = sb("logits", [P, NTILE, NROUT])
        top8 = sb("top8", [P, NTILE, 8])
        top8i = sb("top8i", [P, NTILE, 8], U32)
        topf = sb("topf", [P, TOPK, NTILE])
        sgate_e = sb("sgate_e", [P, NTILE])
        sgate = sb("sgate", [P, NTILE])
        dtop = sb("dtop", [P, NTILE, TOPK])
        psum_p = sb("psum_p", [P, NTILE])
        prec = sb("prec", [P, NTILE])
        pw = sb("pw", [P, NTILE, TOPK])
        resets = sb("resets", [P, BLK])
        rowreset = sb("rowreset", [P, NE, NTILE])
        cnt_i = sb("cnt_i", [P, NE], I32)
        ntl_i = sb("ntl_i", [P, NE], I32)
        ntl = sb("ntl", [P, NE])
        tend = sb("tend", [P, NE])
        tstart = sb("tstart", [P, NE])
        pos = sb("pos", [P, TOPK, NTILE])
        pos_u = sb("pos_u", [P, TOPK, NTILE], U32)
        texp = sb("texp", [P, ETILES])
        texp_u = sb("texp_u", [P, ETILES], U32)

        yout = er_pos[:, :, :].rearrange("p a (t c) -> p a t c", t=2)
        gath_sb = [er_neg[:, :, :].rearrange("p a (t c) -> p (a t) c", t=2),
                   gk[:, :, :].rearrange("p a (t c) -> p (a t) c", t=2)]
        fin = xn

        ld_x = [sem(f"ld_x{i}") for i in range(NBLK)]
        ld_c, ld_mod, ld_wg, ld_wgate, ld_wv, ld_wk, ld_wq, ld_wo, ld_rout, ld_sh, ld_ex = (
            sem(n) for n in ("ld_c", "ld_mod", "ld_wg", "ld_wgate", "ld_wv", "ld_wk", "ld_wq",
                             "ld_wo", "ld_rout", "ld_sh", "ld_ex"))
        xs_zero = sem("xs_zero")
        const_pool, const_dve, zero_ready = sem("const_pool"), sem("const_dve"), sem("zero_ready")
        unit_full = sem("unit_full")
        dve_step, act_step, pool_step = sem("dve_step"), sem("act_step"), sem("pool_step")
        csil_ready, csilb_ready, modc_ready, modr_ready, rows_ready = (
            sem(n) for n in ("csil_ready", "csilb_ready", "modc_ready", "modr_ready", "rows_ready"))
        ln_var, ln_rstd = [sem("ln1_var"), sem("ln2_var")], [sem("ln1_rstd"), sem("ln2_rstd")]
        xn_ready, ht_ready, tt_ready = sem("xn_ready"), sem("ht_ready"), sem("tt_ready")
        zabs_done, zmin_done, zln_done = sem("zabs_done"), sem("zmin_done"), sem("zln_done")
        r_ready, gbase_ready = sem("r_ready"), sem("gbase_ready")
        neg_ready, pos_ready, fac_ready = sem("neg_ready"), sem("pos_ready"), sem("fac_ready")
        sg_ready, v_ready, kh_ready, qeo_ready, qf_ready = (
            sem(n) for n in ("sg_ready", "v_ready", "kh_ready", "qeo_ready", "qf_ready"))
        ktok_ready, kvin_ready, state_ready, decay_ready, tbd_ready = (
            sem(n) for n in ("ktok_ready", "kvin_ready", "state_ready", "decay_ready", "tbd_ready"))
        at_full, atm_ready, set_used = (sem(n) for n in ("at_full", "atm_ready", "set_used"))
        sq_ready, mln_done, rms_ready, m_ready, y_ready = (
            sem(n) for n in ("sq_ready", "mln_done", "rms_ready", "m_ready", "y_ready"))
        woev_done, x1_ready, h2tok_ready, h2T_ready = (
            sem(n) for n in ("woev_done", "x1_ready", "h2tok_ready", "h2T_ready"))
        logit_ready, sge_ready, sgate_ready = sem("logit_ready"), sem("sge_ready"), sem("sgate_ready")
        silu_done, hs_ready, shev_done = sem("silu_done"), sem("hs_ready"), sem("shev_done")
        picked_ready, rank_read, dlog_ready, pexp_ready, posu_ready, texp_ready = (
            sem(n) for n in ("picked_ready", "rank_read", "dlog_ready", "pexp_ready", "posu_ready",
                             "texp_ready"))
        xs_ready, ld_xt, xt_full, xT_ready, up_full, esilu_done, h_ready = (
            sem("xs_ready"), [sem("ld_xt0"), sem("ld_xt1")], sem("xt_full"), sem("xT_ready"),
            sem("up_full"), sem("esilu_done"), sem("h_ready"))
        hTp_full, hTe_ready, down_full, y_out, ys_stored = (
            sem("hTp_full"), sem("hTe_ready"), sem("down_full"), sem("y_out"), [sem("ys_st0"), sem("ys_st1")])
        gath = [sem(f"gath{i}") for i in range(4)]
        comb_done, out_stored = sem("comb_done"), [sem(f"out_stored{i}") for i in range(TPB)]

        def released(key):
            kind, blk, j = key
            return {
                "MODC": [(modc_ready, 2)],
                "MODR": [(modr_ready, 2 * blk + j + 1)],
                "XT": [(ht_ready, 2 * blk + j + 1)],
                "LR": [(tt_ready, blk + 1)],
                "Z": [(zabs_done, 2 * blk + j + 1), (zmin_done, 2 * blk + j + 1)],
                "G": [(sg_ready, 2 * blk + j + 1)],
                "V": [(v_ready, 2 * blk + j + 1)],
                "MS": [(mln_done, 2 * blk + j + 1)],
                "K": [(kh_ready, 2 * blk + j + 1)],
                "WO": [(woev_done, 2 * blk + j + 1)],
                "Q": [(qeo_ready, 4 * blk + 2 * j + 2)],
                "KT": [(ktok_ready, 2 * blk + j + 1)],
                "KV": [(kvin_ready, 2 * blk + j + 1)],
                "HT": [(h2T_ready, 2 * blk + j + 1)],
                "RT": [(logit_ready, blk + 1)],
                "SA": [(silu_done, FTS * blk + j + 1)],
                "SB": [(hs_ready, FTS * blk + j + 1)],
                "RK": [(rank_read, 2)],
                "SD": [(shev_done, 2 * blk + j + 1)],
            }[kind]

        def bank(key):
            return work[TURN[key] % 2]

        def wait_unit(eng, key):
            eng.wait_ge(unit_full, TURN[key] + 1)

        class Steps:

            def __init__(self, eng, s):
                self.eng, self.s, self.n = eng, s, 0

            def did(self, ins):
                self.n += 1
                ins.then_inc(self.s, 1)
                return self.n

            def sync(self):
                self.eng.wait_ge(self.s, self.n)

        block = ctx.enter_context(nc.Block())

        @block.sync
        def _(sp):
            sp.dma_start(x_sb[:, 0:TPB, :], x[0:BLK, :].rearrange("(t p) c -> p t c", p=P)).then_inc(ld_x[0], 16)
            sp.dma_start(csb[:, :, :], cT).then_inc(ld_c, 16)
            sp.dma_start(wmod_sb, wmod.rearrange("(k p) n -> p k n", p=P)).then_inc(ld_mod, 16)
            sp.dma_start(wg1_sb[:, :, :], wg1.rearrange("(k p) n -> p k n", p=P)).then_inc(ld_wg, 16)
            sp.wait_ge(zero_ready, 3)
            sp.dma_start(wg2_sb[0:LOWR, :], wg2).then_inc(ld_wg, 16)
            sp.dma_start(wg2_sb[32:33, :], bg2.rearrange("(a n) -> a n", a=1)).then_inc(ld_wg, 16)
            for w_sb, w, s in ((wgate_sb, wgate, ld_wgate), (wv_sb, wv, ld_wv), (wk_sb, wk, ld_wk),
                               (wq_sb, wq, ld_wq)):
                sp.dma_start(w_sb[:, :, :], w.rearrange("(k p) n -> p k n", p=P)).then_inc(s, 16)
            for i in range(1, NBLK):
                sp.dma_start(x_sb[:, i * TPB:(i + 1) * TPB, :],
                             x[i * BLK:(i + 1) * BLK, :].rearrange("(t p) c -> p t c", p=P)).then_inc(ld_x[i], 16)
            sp.dma_start(wo_sb[:, :, :], wo.rearrange("(k p) n -> p k n", p=P)).then_inc(ld_wo, 16)
            for h in range(P // HEAD):
                sp.dma_start(nw_sb[h * HEAD:(h + 1) * HEAD, :],
                             norm_w.rearrange("(p a) -> p a", a=1)).then_inc(ld_wo, 16)
            sp.dma_start(rout_sb[:, :, :], router.rearrange("(k p) n -> p k n", p=P)).then_inc(ld_rout, 16)
            sp.dma_start(sup_sb[:, :, :, :].rearrange("p k a f -> p k (a f)"),
                         s_up.rearrange("(k p) n -> p k n", p=P)).then_inc(ld_sh, 16)
            sp.dma_start(sdn_sb[:, 0:FTS - 1, :],
                         s_down[0:(FTS - 1) * P, :].rearrange("(f p) n -> p f n", p=P)).then_inc(ld_sh, 16)
            sp.dma_start(sdn_sb[0:FS - (FTS - 1) * P, FTS - 1, :], s_down[(FTS - 1) * P:FS, :]).then_inc(ld_sh, 16)
            sp.wait_ge(zero_ready, 6)
            for i in range(ETILES // 4):
                sp.dma_start(xs_dram[i * BLK:(i + 1) * BLK, :].rearrange("(t p) c -> p t c", p=P),
                             atm_zero).then_inc(xs_zero, 16)
            sp.wait_ge(set_used, 2 * NBLK)
            for e in range(NE):
                sp.dma_start(eup[:, e, :, :], e_up[e].rearrange("(k p) n -> p k n", p=P)).then_inc(ld_ex, 16)
                sp.dma_start(edn[0:FEH, e, :, :], e_down[e].rearrange("(k p) n -> p k n", p=FEH)).then_inc(ld_ex, 16)
            sp.wait_ge(xs_ready, 16 * TOPK * NTILE)

            def load_pair(q, slot):
                sp.dma_start(xt[:, slot, :, :],
                             xs_dram[bass.ds(q * (2 * P), 2 * P), :].rearrange("(t p) c -> p t c", p=P)
                             ).then_inc(ld_xt[slot], 16)

            def store_pair(q, slot):
                sp.wait_ge(y_out, q * 2 + 2)
                sp.dma_start(ys_dram[bass.ds(q * (2 * P), 2 * P), :].rearrange("(t p) c -> p t c", p=P),
                             yout[:, slot, :, :]).then_inc(ys_stored[slot], 16)

            def load_store(q, slot):
                sp.wait_ge(xt_full, q * 2 - 2)
                load_pair(q, slot)
                store_pair(q - 2, slot)

            load_pair(0, 0)
            load_pair(1, 1)
            with sp.Fori(1, ETILES // EGRP) as grp:
                load_store(grp * 2, 0)
                load_store(grp * 2 + 1, 1)
            for slot in range(2):
                store_pair(ETILES // 2 - 2 + slot, slot)
            for t in range(NTILE):
                sp.wait_ge(comb_done, t + 1)
                sp.dma_start(out[t * P:(t + 1) * P, :], fin[:, t % TPB, :]).then_inc(out_stored[t % TPB], 16)
            for s in out_stored:
                sp.wait_ge(s, 16 * (NTILE // TPB))

        @block.gpsimd
        def _(pool):
            g = nc.gpsimd
            steps = Steps(pool, pool_step)
            steps.did(g.memset(tT[:, :], 0.0))
            g.memset(wg2_sb[:, :], 0.0).then_inc(zero_ready, 1)
            steps.sync()
            pool.wait_ge(zero_ready, 1)
            g.memset(tT[32:33, :], 1.0).then_inc(zero_ready, 1)
            pool.wait_ge(zero_ready, 2)
            g.memset(eps_c[:, :], EPS).then_inc(zero_ready, 1)
            g.memset(vpad, 0.0).then_inc(zero_ready, 1)
            g.memset(tbd, 0.0).then_inc(zero_ready, 1)
            g.memset(atm, 0.0).then_inc(zero_ready, 1)
            steps.did(g.memset(decay[:, :, :, :], 0.0))
            steps.did(g.memset(ident[:, :], 0.0))
            for m in (ones, tri, bd16, causal):
                steps.did(g.memset(m[:, :] if m is not causal else m[:, :, :], 1.0 if m is not bd16 else 1.0 / HEAD))
            steps.did(g.memset(rowreset[:, :, :], 1.0))
            steps.did(g.memset(resets[:, :], 1.0))
            steps.sync()
            steps.did(g.affine_select(out=ident[:, :], in_=ident[:, :], compare_op=ALU.not_equal, fill=1.0,
                                      base=0, pattern=[[-1, P]], channel_multiplier=1))
            steps.did(g.affine_select(out=tri[:, :], in_=tri[:, :], compare_op=ALU.is_gt, fill=0.0,
                                      base=0, pattern=[[1, P]], channel_multiplier=-1))
            bd_v = bd16[:, :].rearrange("p (h v) -> p h v", v=HEAD)
            steps.did(g.affine_select(out=bd_v, in_=bd_v, compare_op=ALU.is_ge, fill=0.0,
                                      base=0, pattern=[[-HEAD, P // HEAD], [0, HEAD]], channel_multiplier=1))
            steps.sync()
            steps.did(g.affine_select(out=bd_v, in_=bd_v, compare_op=ALU.is_ge, fill=0.0,
                                      base=HEAD - 1, pattern=[[HEAD, P // HEAD], [0, HEAD]], channel_multiplier=-1))
            for e in range(2):
                half = causal[CHUNK * e:CHUNK * (e + 1), :, :]
                steps.sync()
                steps.did(g.affine_select(out=half, in_=half, compare_op=ALU.is_ge, fill=0.0,
                                          base=0, pattern=[[0, 2 * NPAIR], [1, CHUNK]], channel_multiplier=-1))
            steps.sync()
            steps.did(g.memset(rowreset[:, :, 0:1], 0.0))
            steps.did(g.memset(resets[:, :].rearrange("p (c l) -> p c l", l=CHUNK)[:, :, 0:1], 0.0))
            steps.did(g.iota(iota_i[:, :], [[1, ETILES]], base=0, channel_multiplier=0))
            steps.sync()
            for j in range(NPAIR):
                q = slice(32 * j, 32 * j + 32)
                steps.did(g.tensor_scalar(pmask[q, :], bd16[q, 32 * j:32 * j + 32], float(HEAD), None, ALU.mult))
                steps.sync()
            g.tensor_scalar(qsel[:, :], pmask[:, :].rearrange("p (h v) -> p h v", v=HEAD)[:, :, 0], SCALE, None,
                            ALU.mult).then_inc(const_pool, 1)

            def tokens_of_chunks(ap, e):
                return ap.rearrange("p g (t h l) -> p g t h l", t=TPB, h=2)[:, :, :, e, :]

            for s in range(NBLK + 1):
                if s >= 1:
                    b = s - 1
                    for e in range(2):
                        pool.wait_ge(rms_ready, 2 * b + e + 1)
                        if e == 0:
                            pool.wait_ge(sg_ready, 2 * b + 2)
                        m = sq[:, e, :].rearrange("p (g t l) -> p g t l", g=KC, t=TPB)
                        g.tensor_tensor(m, m, tokens_of_chunks(sg[:, b % 2, :, :], e), ALU.mult).then_inc(m_ready, 1)
                if s < NBLK:
                    for gr in range(KC):
                        pool.wait_ge(qeo_ready, 4 * s + 2 * gr + 2)
                        g.tensor_tensor(qf[:, gr, :].rearrange("p (c l) -> p c l", c=CPB), qeo[:, gr, :, 0, :],
                                        qeo[:, gr, :, 1, :], ALU.add).then_inc(qf_ready, 1)
                    pool.wait_ge(fac_ready, 2 * s + 2)
                    if s >= 1:
                        pool.wait_ge(state_ready, s)
                    k = steps.did(g.tensor_tensor(f_all[:, :, :], f_base[:, :, :], f_last[:, :, :], ALU.mult))
                    steps.sync()
                    for gr in range(KC):
                        g.tensor_copy(decay[:, gr, :, 1:CPB],
                                      f_all[:, gr, 1:CPB].unsqueeze(1).broadcast_to([P, 32, CPB - 1])).then_inc(decay_ready, 1)
                    steps.did(g.tensor_tensor(
                        tmask[:, :, :, :], f_base[:, :, :].unsqueeze(3).broadcast_to([P, KC, CPB, 32]),
                        free_dims(pmask[:, :], [[0, KC], [0, CPB], [1, 32]]), ALU.mult))
                    steps.sync()
                    pool.wait_ge(state_ready, s + 1)
                    first = 1 if s % BPB == 0 else 0
                    for j in range(NPAIR):
                        q = slice(32 * j, 32 * j + 32)
                        ins = g.tensor_tensor(
                            tbd[q, :, 1:CPB, 32 * j:32 * j + 32],
                            state[q, s % 2, :, :, 0:CPB - 1].rearrange("p g v c -> p g c v"),
                            tmask[q, :, 1:CPB, :], ALU.mult)
                        if not first:
                            steps.did(ins)
                            steps.sync()
                            ins = g.tensor_tensor(tbd[q, :, 0, 32 * j:32 * j + 32], state[q, 1 - s % 2, :, :, CPB - 1],
                                                  tmask[q, :, 0, :], ALU.mult)
                        ins.then_inc(tbd_ready, 1)
                        pool.wait_ge(tbd_ready, NPAIR * s + j + 1)

            pool.wait_ge(xs_zero, 16 * (ETILES // 4))
            pool.wait_ge(posu_ready, 1)
            pool.wait_ge(h2tok_ready, NBLK)
            for k in range(TOPK):
                for t in range(NTILE):
                    g.indirect_dma_start(out=xs_dram, out_offset=bass.IndirectOffsetOnAxis(ap=pos_u[:, k, t:t + 1], axis=0),
                                         in_=h2tok[:, t, :], in_offset=None).then_inc(xs_ready, 16)
            for s in ys_stored:
                pool.wait_ge(s, 16 * (ETILES // 4))
            for t in range(NTILE):
                if t >= 4:
                    pool.wait_ge(comb_done, t - 3)
                for k in range(TOPK):
                    g.indirect_dma_start(out=gath_sb[k][:, t % 4, :], out_offset=None, in_=ys_dram,
                                         in_offset=bass.IndirectOffsetOnAxis(ap=pos_u[:, k, t:t + 1], axis=0)
                                         ).then_inc(gath[t % 4], 16)

        def shared_act(act, a, blk):
            if blk >= 1:
                act.wait_ge(shev_done, 2 * blk)
            for f, (_, m) in enumerate(SH_F):
                wait_unit(act, ("SA", blk, f))
                a.activation(hs[0:m, f, :], bank(("SA", blk, f))[0:m, :], ACT.Silu).then_inc(silu_done, 1)

        @block.scalar
        def _(act):
            a = nc.scalar
            steps = Steps(act, act_step)
            act.wait_ge(ld_c, 16)
            a.activation(csil[:, :, :], csb[:, :, :], ACT.Silu).then_inc(csil_ready, 1)
            act.wait_ge(zero_ready, 3)

            def rstd_of(which, n, at):
                act.wait_ge(ln_var[which], n)
                steps.did(a.activation(lnv[:, which, :], mv[:, which, :, 1], ACT.Ln, bias=eps_c[:, 0:1]))
                steps.sync()
                a.activation(rstd[:, which, :], lnv[:, which, :], ACT.Exp, scale=-0.5).then_inc(ln_rstd[which], 1)

            rstd_of(0, 1, 0)
            for b in range(BATCH):
                for h in range(2):
                    wait_unit(act, ("MODR", b, h))
                    a.activation(rows[:, b, 2 * h:2 * h + 2, :].rearrange("p a n -> p (a n)"),
                                 bank(("MODR", b, h))[:, :], ACT.Copy).then_inc(modr_ready, 1)
            for s in range(NBLK + 1):
                b = s - 1
                if s < NBLK:
                    row = s // BPB
                    if s == 0:
                        act.wait_ge(modc_ready, 2)
                    for k in range(KC):
                        wait_unit(act, ("XT", s, k))
                        a.activation(hT[:, k, :], bank(("XT", s, k))[:, :], ACT.Identity,
                                     bias=cols[:, 0, k, row:row + 1], scale=cols[:, 1, k, row:row + 1]).then_inc(ht_ready, 1)
                    wait_unit(act, ("LR", s, 0))
                    a.activation(tT[0:LOWR, :], bank(("LR", s, 0))[0:LOWR, :], ACT.Copy).then_inc(tt_ready, 1)
                    for gr in range(KC):
                        wait_unit(act, ("Z", s, gr))
                        a.activation(za[:, gr, :], bank(("Z", s, gr))[:, :], ACT.Abs).then_inc(zabs_done, 1)
                    act.wait_ge(zabs_done, 2 * s + 2)
                    steps.did(a.activation(za[:, :, :], za[:, :, :], ACT.Exp, scale=-1.0))
                    steps.sync()
                    a.activation(za[:, :, :], za[:, :, :], ACT.Ln, bias=1.0).then_inc(zln_done, 1)
                    if s >= 2:
                        act.wait_ge(m_ready, 2 * (s - 1))
                    for gr in range(KC):
                        wait_unit(act, ("G", s, gr))
                        a.activation(sg[:, s % 2, gr, :], bank(("G", s, gr))[:, :], ACT.Silu).then_inc(sg_ready, 1)
                if s >= 1:
                    act.wait_ge(set_used, 2 * b + 2)
                    for e in range(2):
                        if b >= 1:
                            act.wait_ge(y_ready, 2 * b)
                        a.activation(sq[:, e, :], o_ps[e][:, :], ACT.Square).then_inc(sq_ready, 1)
                if s < NBLK:
                    if s == 0:
                        act.wait_ge(zero_ready, 4)
                    for jj in range(2):
                        wait_unit(act, ("V", s, jj))
                        for t in range(2):
                            ins = a.activation(free_dims(vpad[:, 2 * jj + t, 0, 0:1], [[64, KC * NPAIR], [48, 2], [1, HEAD]]),
                                               bank(("V", s, jj))[:, t * HID:(t + 1) * HID]
                                               .rearrange("p (r h v) -> p r h v", h=2, v=HEAD), ACT.Copy)
                        ins.then_inc(v_ready, 1)
                    for gr in range(KC):
                        act.wait_ge(r_ready, 2 * s + gr + 1)
                        if s >= 1 and gr == 0:
                            act.wait_ge(qeo_ready, 4 * s)
                        a.activation(er_neg[:, gr, :], gk[:, gr, :], ACT.Exp, scale=-1.0 / GATE_NORM).then_inc(neg_ready, 1)
                    for gr in range(KC):
                        a.activation(er_pos[:, gr, :], gk[:, gr, :], ACT.Exp, scale=1.0 / GATE_NORM).then_inc(pos_ready, 1)
                    if s >= 1:
                        act.wait_ge(tbd_ready, NPAIR * s)
                        act.wait_ge(state_ready, s)
                    a.activation(f_base[:, :, :], gbase[:, :, :], ACT.Exp, scale=1.0 / GATE_NORM).then_inc(fac_ready, 1)
                    a.activation(f_last[:, :, :], gk[:, :, :].rearrange("p g (c l) -> p g c l", c=CPB)[:, :, :, CHUNK - 1],
                                 ACT.Exp, scale=1.0 / GATE_NORM).then_inc(fac_ready, 1)
                if s >= 1:
                    for e in range(2):
                        wait_unit(act, ("MS", b, e))
                        a.activation(sq[:, e, :], bank(("MS", b, e))[:, :], ACT.Ln, bias=eps_c[:, 0:1]).then_inc(mln_done, 1)
                    for e in range(2):
                        act.wait_ge(mln_done, 2 * b + e + 1)
                        a.activation(sq[:, e, :], sq[:, e, :], ACT.Exp, scale=-0.5).then_inc(rms_ready, 1)
                if s < NBLK:
                    for gr in range(KC):
                        wait_unit(act, ("KT", s, gr))
                        a.activation(ktok[:, :, gr, :], bank(("KT", s, gr))[:, :].rearrange("p (t c) -> p t c", t=TPB),
                                     ACT.Copy).then_inc(ktok_ready, 1)
                if s >= 1:
                    rstd_of(1, s, b)
                    for k in range(KC):
                        wait_unit(act, ("HT", b, k))
                        a.activation(h2T[:, b % 2, k, :], bank(("HT", b, k))[:, :], ACT.Copy).then_inc(h2T_ready, 1)
                if s + 1 < NBLK:
                    rstd_of(0, s + 2, 0)
                if s >= 1:
                    act.wait_ge(logit_ready, b + 1)
                    a.activation(sgate_e[:, b * TPB:(b + 1) * TPB], logits[:, b * TPB:(b + 1) * TPB, NE], ACT.Exp,
                                 scale=-1.0).then_inc(sge_ready, 1)
                if s == NBLK:
                    act.wait_ge(dlog_ready, 2)
                    steps.did(a.activation(dlog[:, :, :], dlog[:, :, :], ACT.Exp))
                    steps.did(a.activation(pw[:, :, :], dtop[:, :, :], ACT.Exp))
                    steps.sync()
                    a.activation(dtop[:, :, :], dtop[:, :, :], ACT.Copy).then_inc(pexp_ready, 1)
                for blk in SHARED_AFTER.get(s, ()):
                    shared_act(act, a, blk)

            def evac_rows(i, u):
                act.wait_ge(xt_full, i + 1)
                a.activation(xT[:, u % 2, :], at_ps[u % 2][:, 0:KC * P], ACT.Copy).then_inc(xT_ready, 1)

            def expert_silu(i, u):
                act.wait_ge(up_full, i + 1)
                a.activation(esil[:, u % 2, :], at_ps[2 + u % 2][:, 0:FE], ACT.Silu).then_inc(esilu_done, 1)

            evac_rows(0, 0)

            def group(i0, last=False):
                for u in range(EGRP):
                    expert_silu(i0 + u, u)
                    if not (last and u == EGRP - 1):
                        evac_rows(i0 + u + 1, u + 1)

            with act.Fori(0, ETILES // EGRP - 1) as grp:
                group(grp * EGRP)
            group(ETILES - EGRP, last=True)
            shared_act(act, a, NBLK - 1)

        def routing_a(dve, v, steps):
            dve.wait_ge(const_pool, 1)
            steps.did(v.tensor_copy(iota_f[:, :], iota_i[:, :]))
            steps.did(v.tensor_copy(topf[:, :, :], top8i[:, :, 0:TOPK].rearrange("p t k -> p k t")))
            steps.sync()
            for k in range(TOPK):
                steps.did(v.tensor_tensor(onehot[:, k, :, :], iota_f[:, 0:NE].unsqueeze(1).broadcast_to([P, NTILE, NE]),
                                          topf[:, k, :].unsqueeze(2).broadcast_to([P, NTILE, NE]), ALU.is_equal))
            steps.sync()
            v.tensor_tensor(picked[:, :, :], onehot[:, 0, :, :], onehot[:, 1, :, :], ALU.add).then_inc(picked_ready, 1)
            v.tensor_tensor(dlog[:, :, :], logits[:, :, 0:NE], top8[:, :, 0:1].broadcast_to([P, NTILE, NE]),
                            ALU.subtract).then_inc(dlog_ready, 1)
            v.tensor_tensor(dtop[:, :, :], top8[:, :, 0:TOPK], top8[:, :, 0:1].broadcast_to([P, NTILE, TOPK]),
                            ALU.subtract).then_inc(dlog_ready, 1)

        def routing_b(dve, v, steps):
            key = ("RK", 0, 0)
            wait_unit(dve, key)
            te = bank(key)[:, P:2 * P].rearrange("p (t e) -> p e t", t=NTILE)
            v.tensor_copy(tot[:, :, :], te).then_inc(rank_read, 1)
            dve.wait_ge(rank_read, 1)
            steps.did(v.tensor_tensor_scan(incl[:, :, :].rearrange("p e t -> p (e t)"),
                                           rowreset[:, :, :].rearrange("p e t -> p (e t)"),
                                           tot[:, :, :].rearrange("p e t -> p (e t)"), 0.0, ALU.mult, ALU.add))
            steps.sync()
            steps.did(v.tensor_scalar(cnt_i[:, :], incl[:, :, NTILE - 1], float(P - 1), None, ALU.add))
            steps.did(v.tensor_tensor(base[:, :, :], incl[:, :, :], tot[:, :, :], ALU.subtract))
            steps.sync()
            steps.did(v.tensor_scalar(ntl_i[:, :], cnt_i[:, :], 7, None, ALU.arith_shift_right))
            steps.sync()
            steps.did(v.tensor_copy(ntl[:, :], ntl_i[:, :]))
            steps.sync()
            steps.did(v.tensor_tensor_scan(tend[:, :], ones[:, 0:NE], ntl[:, :], 0.0, ALU.mult, ALU.add))
            steps.sync()
            steps.did(v.tensor_tensor(tstart[:, :], tend[:, :], ntl[:, :], ALU.subtract))
            steps.did(v.tensor_tensor(tge[:, :, :], iota_f[:, :].unsqueeze(2).broadcast_to([P, ETILES, NE]),
                                      tend[:, :].unsqueeze(1).broadcast_to([P, ETILES, NE]), ALU.is_ge))
            steps.sync()
            steps.did(v.tensor_reduce(texp[:, :], tge[:, :, :], AX_X, ALU.add))
            steps.did(v.tensor_scalar(tstart[:, :], tstart[:, :], float(P), None, ALU.mult))
            steps.sync()
            v.tensor_scalar(texp_u[:, :], texp[:, :], float(NE - 1), None, ALU.min).then_inc(texp_ready, 1)
            steps.did(v.tensor_tensor(base[:, :, :], base[:, :, :], tstart[:, :].unsqueeze(2).broadcast_to([P, NE, NTILE]), ALU.add))
            steps.sync()
            v.tensor_tensor(posf[:, :, :], bank(key)[:, 0:P].rearrange("p (t e) -> p t e", t=NTILE),
                            base[:, :, :].rearrange("p e t -> p t e"), ALU.add).then_inc(rank_read, 1)
            dve.wait_ge(rank_read, 2)
            for k in range(TOPK):
                steps.did(v.tensor_tensor(pprod[:, :, :], onehot[:, k, :, :], posf[:, :, :], ALU.mult))
                steps.sync()
                steps.did(v.tensor_reduce(pos[:, k, :], pprod[:, :, :], AX_X, ALU.add))
                steps.sync()
            v.tensor_copy(pos_u[:, :, :], pos[:, :, :]).then_inc(posu_ready, 1)
            dve.wait_ge(pexp_ready, 1)
            steps.did(v.tensor_reduce(psum_p[:, :], dlog[:, :, :], AX_X, ALU.add))
            steps.sync()
            steps.did(v.reciprocal(prec[:, :], psum_p[:, :]))
            steps.sync()
            steps.did(v.tensor_tensor(pw[:, :, :], pw[:, :, :], prec[:, :].unsqueeze(2).broadcast_to([P, NTILE, TOPK]), ALU.mult))
            steps.sync()

        @block.vector
        def _(dve):
            v = nc.vector
            steps = Steps(dve, dve_step)

            def ln_stats(which, tile0):
                for t in range(TPB):
                    steps.did(v.bn_stats(stats[:, which, t, :], x_sb[:, tile0 + t, :]))
                steps.sync()
                for t in range(TPB - 1):
                    steps.did(v.bn_aggr(mv[:, which, t, :], stats[:, which, t, :]))
                steps.sync()
                v.bn_aggr(mv[:, which, TPB - 1, :], stats[:, which, TPB - 1, :]).then_inc(ln_var[which], 1)

            def ln_rows(which, n, dst, tile0, last_sem):
                dve.wait_ge(ln_rstd[which], n)
                steps.did(v.scalar_tensor_tensor(out=nmr[:, which, :], in0=mv[:, which, :, 0], scalar=-1.0,
                                                 in1=rstd[:, which, :], op0=ALU.mult, op1=ALU.mult))
                steps.sync()
                for t in range(TPB):
                    ins = v.tensor_scalar(dst[:, t, :], x_sb[:, tile0 + t, :], rstd[:, which, t:t + 1],
                                          nmr[:, which, t:t + 1], ALU.mult, ALU.add)
                    if last_sem is not None and t == TPB - 1:
                        ins.then_inc(last_sem, 1)
                    else:
                        steps.did(ins)

            dve.wait_ge(ld_x[0], 16)
            ln_stats(0, 0)
            dve.wait_ge(csil_ready, 1)
            v.tensor_copy(csil_b[:, :, :, :], csil[:, :, :].unsqueeze(3).broadcast_to([P, KC, BATCH, P])).then_inc(csilb_ready, 1)
            ln_rows(0, 1, xn, 0, xn_ready)
            steps.sync()
            wait_unit(dve, ("MODC", 0, 0))
            modc = bank(("MODC", 0, 0))[:, 0:4 * BATCH].rearrange("p (w k b) -> p w k b", w=2, k=KC)
            v.tensor_copy(cols[:, 0, :, :], modc[:, 0, :, :]).then_inc(modc_ready, 1)
            v.tensor_scalar(cols[:, 1, :, :], modc[:, 1, :, :], 1.0, None, ALU.add).then_inc(modc_ready, 1)
            dve.wait_ge(modr_ready, 4)
            for w in (GA, GB):
                gv = rows[:, :, w, :]
                steps.did(v.tensor_scalar(sgn[:, :, :], gv, 0.0, 2.0, ALU.is_ge, ALU.mult))
                steps.did(v.tensor_scalar(mag[:, :, :], gv, -1.0, None, ALU.mult))
                steps.sync()
                steps.did(v.tensor_tensor(mag[:, :, :], mag[:, :, :], gv, ALU.max))
                steps.sync()
                steps.did(v.tensor_scalar(mag[:, :, :], mag[:, :, :], 0.25, None, ALU.max))
                steps.sync()
                steps.did(v.scalar_tensor_tensor(out=gv, in0=sgn[:, :, :], scalar=-1.0, in1=mag[:, :, :],
                                                 op0=ALU.add, op1=ALU.mult))
                steps.sync()
            steps.did(v.tensor_scalar(rows[:, :, CB1, :], rows[:, :, CB1, :], 1.0, None, ALU.add))
            dve.wait_ge(ld_wo, 16 * 9)
            for k in range(KC):
                steps.did(v.tensor_scalar(wo_sb[:, k, :], wo_sb[:, k, :], nw_sb[:, 0:1], None, ALU.mult))
            steps.sync()
            v.engine_nop().then_inc(rows_ready, 1)

            def shared_mult(blk, between=None):
                for f, (_, m) in enumerate(SH_F):
                    if between:
                        between(f)
                    dve.wait_ge(silu_done, FTS * blk + f + 1)
                    wait_unit(dve, ("SB", blk, f))
                    v.tensor_tensor(hs[0:m, f, :], bank(("SB", blk, f))[0:m, :], hs[0:m, f, :],
                                    ALU.mult).then_inc(hs_ready, 1)

            def shared_add(blk):
                for jj in range(2):
                    wait_unit(dve, ("SD", blk, jj))
                    if jj:
                        steps.sync()
                    for t in range(2):
                        tile = blk * TPB + 2 * jj + t
                        ins = v.scalar_tensor_tensor(
                            out=tmp[:, t, :], in0=bank(("SD", blk, jj))[:, t * HID:(t + 1) * HID],
                            scalar=sgate[:, tile:tile + 1], in1=rows[:, blk // BPB, GB, :], op0=ALU.mult, op1=ALU.mult)
                        if t:
                            ins.then_inc(shev_done, 1)
                        else:
                            steps.did(ins)
                    dve.wait_ge(shev_done, 2 * blk + jj + 1)
                    steps.sync()
                    xv = x_sb[:, blk * TPB + 2 * jj:blk * TPB + 2 * jj + 2, :]
                    steps.did(v.tensor_tensor(xv, xv, tmp[:, :, :], ALU.add))
                steps.sync()

            dve.wait_ge(const_pool, 1)
            for s in range(NBLK + 1):
                b = s - 1
                if s < NBLK:
                    if s >= 1:
                        dve.wait_ge(pos_ready, 2 * s)
                        dve.wait_ge(fac_ready, 2 * s)
                    for gr in range(KC):
                        wait_unit(dve, ("Z", s, gr))
                        if gr == 0:
                            dve.wait_ge(zabs_done, 2 * s + 1)
                        else:
                            dve.wait_ge(zabs_done, 2 * s + 2)
                        v.tensor_scalar(gk[:, gr, :], bank(("Z", s, gr))[:, :], 0.0, None, ALU.min).then_inc(zmin_done, 1)
                    dve.wait_ge(zln_done, s + 1)
                    for gr in range(KC):
                        dve.wait_ge(zmin_done, 2 * s + gr + 1)
                        steps.did(v.tensor_tensor(gk[:, gr, :], gk[:, gr, :], za[:, gr, :], ALU.subtract))
                        steps.sync()
                        starts = gk[:, gr, :].rearrange("p (c l) -> p c l", c=CPB)[:, :, 0]
                        v.tensor_copy(gbase[:, gr, :], starts).then_inc(gbase_ready, 1)
                        dve.wait_ge(gbase_ready, 2 * s + gr + 1)
                        steps.did(v.memset(starts, 0.0))
                        steps.sync()
                        v.tensor_tensor_scan(gk[:, gr, :], resets[:, :], gk[:, gr, :], 0.0,
                                             ALU.mult, ALU.add).then_inc(r_ready, 1)
                if s >= 1:
                    if s == 1:
                        dve.wait_ge(xs_zero, 16 * (ETILES // 4))
                        dve.wait_ge(zero_ready, 6)
                    for n in (2 * b, 2 * b + 1):
                        if n >= 2:
                            dve.wait_ge(set_used, n - 1)
                        for j in range(NPAIR):
                            dve.wait_ge(at_full, NPAIR * n + j + 1)
                            v.copy_predicated(atm[:, n % 2, j, :], causal[:, :, :].bitcast(U32).rearrange("p r l -> p (r l)"),
                                              at_ps[j][:, :]).then_inc(atm_ready, 1)
                if s < NBLK:
                    for gr in range(KC):
                        wait_unit(dve, ("K", s, gr))
                        dve.wait_ge(neg_ready, 2 * s + gr + 1)
                        v.tensor_tensor(kh[:, gr, :], bank(("K", s, gr))[:, :], er_neg[:, gr, :], ALU.mult).then_inc(kh_ready, 1)
                if s >= 1:
                    for e in range(2):
                        dve.wait_ge(m_ready, 2 * b + e + 1)
                        ov = o_ps[e][:, :].rearrange("p (g t l) -> p g t l", g=KC, t=TPB)
                        yv = yT[:, :, :].rearrange("p g (t h l) -> p g t h l", t=TPB, h=2)[:, :, :, e, :]
                        v.tensor_tensor(yv, ov, sq[:, e, :].rearrange("p (g t l) -> p g t l", g=KC, t=TPB),
                                        ALU.mult).then_inc(y_ready, 1)
                    for jj in range(2):
                        wait_unit(dve, ("WO", b, jj))
                        steps.sync()
                        ga2 = rows[:, b // BPB, GA, :].unsqueeze(1).broadcast_to([P, 2, HID])
                        v.tensor_tensor(tmp[:, :, :], bank(("WO", b, jj))[:, :].rearrange("p (t c) -> p t c", t=2), ga2,
                                        ALU.mult).then_inc(woev_done, 1)
                        dve.wait_ge(woev_done, 2 * b + jj + 1)
                        xv = x_sb[:, b * TPB + 2 * jj:b * TPB + 2 * jj + 2, :]
                        steps.did(v.tensor_tensor(xv, xv, tmp[:, :, :], ALU.add))
                if s < NBLK:
                    for gr in range(KC):
                        wait_unit(dve, ("Q", s, gr))
                        dve.wait_ge(pos_ready, 2 * s + gr + 1)
                        for h in range(2):
                            v.scalar_tensor_tensor(
                                out=qeo[:, gr, :, h, :], in0=bank(("Q", s, gr))[:, :].rearrange("p (c l) -> p c l", c=CPB),
                                scalar=qsel[:, h:h + 1], in1=er_pos[:, gr, :].rearrange("p (c l) -> p c l", c=CPB),
                                op0=ALU.mult, op1=ALU.mult).then_inc(qeo_ready, 1)
                if s >= 1:
                    steps.sync()
                    ln_stats(1, b * TPB)
                if s < NBLK:
                    dve.wait_ge(fac_ready, 2 * s + 2)
                    if s >= 1:
                        steps.sync()
                    kv_v = kv_in[:, :, :, :].rearrange("p g v (t h) -> p g t h v", h=2)
                    for e in range(2):
                        wait_unit(dve, ("KV", s, e))
                        fl = f_last[:, :, :].rearrange("p g (t h) -> p g t h", h=2)[:, :, :, e]
                        v.tensor_tensor(kv_v[:, :, :, e, :], bank(("KV", s, e))[:, 0:256].rearrange("p (g t v) -> p g t v", g=KC, t=TPB),
                                        fl.unsqueeze(3).broadcast_to([P, KC, TPB, 32]), ALU.mult).then_inc(kvin_ready, 1)
                    dve.wait_ge(kvin_ready, 2 * s + 2)
                    dve.wait_ge(decay_ready, 2 * s + 2)
                    if s % BPB:
                        steps.did(v.tensor_tensor(carry[:, :, :], state[:, 1 - s % 2, :, :, CPB - 1],
                                                  f_all[:, :, 0:1].broadcast_to([P, KC, 32]), ALU.mult))
                        steps.sync()
                        steps.did(v.tensor_tensor(kv_in[:, :, :, 0], kv_in[:, :, :, 0], carry[:, :, :], ALU.add))
                        steps.sync()
                    if s >= 1:
                        dve.wait_ge(tbd_ready, NPAIR * s)
                    v.tensor_tensor_scan(state[:, s % 2, :, :, :].rearrange("p g v c -> p (g v c)"),
                                         decay[:, :, :, :].rearrange("p g v c -> p (g v c)"),
                                         kv_in[:, :, :, :].rearrange("p g v c -> p (g v c)"), 0.0,
                                         ALU.mult, ALU.add).then_inc(state_ready, 1)
                if s >= 1:
                    ln_rows(1, s, xn2, b * TPB, None)
                    steps.sync()
                    ht = h2tok[:, b * TPB:(b + 1) * TPB, :]
                    bc = [rows[:, b // BPB, w, :].unsqueeze(1).broadcast_to([P, TPB, HID]) for w in (CB1, SB_)]
                    steps.did(v.tensor_tensor(xn2[:, :, :], xn2[:, :, :], bc[0], ALU.mult))
                    steps.sync()
                    v.tensor_tensor(ht, xn2[:, :, :], bc[1], ALU.add).then_inc(h2tok_ready, 1)
                if s + 1 < NBLK:
                    dve.wait_ge(ld_x[s + 1], 16)
                    ln_stats(0, (s + 1) * TPB)
                    wait_unit(dve, ("XT", s, 1))
                    ln_rows(0, s + 2, xn, (s + 1) * TPB, xn_ready)
                if s == 0:
                    continue
                tl = slice(b * TPB, (b + 1) * TPB)
                wait_unit(dve, ("RT", b, 0))
                v.tensor_copy(logits[:, tl, :], bank(("RT", b, 0))[:, 0:TPB * NROUT].rearrange("p (t e) -> p t e", t=TPB)
                              ).then_inc(logit_ready, 1)
                dve.wait_ge(logit_ready, b + 1)
                for t in range(b * TPB, (b + 1) * TPB):
                    steps.did(v.max(top8[:, t, :], logits[:, t, 0:NE]))
                steps.sync()
                for t in range(b * TPB, (b + 1) * TPB):
                    steps.did(v.max_index(top8i[:, t, :], top8[:, t, :], logits[:, t, 0:NE]))
                dve.wait_ge(sge_ready, b + 1)
                steps.did(v.tensor_scalar(sgate[:, tl], sgate_e[:, tl], 1.0, None, ALU.add))
                steps.sync()
                steps.did(v.reciprocal(sgate[:, tl], sgate[:, tl]))
                steps.sync()
                if s == NBLK:
                    routing_a(dve, v, steps)
                for blk in SHARED_AFTER.get(s, ()):
                    shared_mult(blk)
                    if blk == RANK_IN:
                        routing_b(dve, v, steps)
                    shared_add(blk)

            def expert_h(i, u):
                dve.wait_ge(esilu_done, i + 1)
                v.tensor_tensor(esil[:, u % 2, :], at_ps[2 + u % 2][:, FE:2 * FE], esil[:, u % 2, :],
                                ALU.mult).then_inc(h_ready, 1)

            def evac_hT(i, u):
                dve.wait_ge(hTp_full, i + 1)
                v.tensor_copy(hTe[0:FEH, u % 2, :], o_ps[u % 2][0:FEH, 0:2 * P]).then_inc(hTe_ready, 1)

            def evac_y(i, u):
                dve.wait_ge(down_full, i + 1)
                v.tensor_copy(yout[:, (u // 2) % 2, u % 2, :], work[u % 2][:, 0:HID]).then_inc(y_out, 1)

            def group(i0, first=False):
                for u in range(EGRP):
                    expert_h(i0 + u, u)
                    if not (first and u == 0):
                        if not first and u in (1, 3):
                            slot = 0 if u == 1 else 1
                            dve.wait_ge(ys_stored[slot], stored_before(i0, slot))
                        evac_y(i0 + u - 1, (u - 1) % EGRP)
                    evac_hT(i0 + u, u)

            def stored_before(i0, slot):
                return 16 * (i0 // EGRP) if isinstance(i0, int) else i0 * (16 // EGRP)

            group(0, first=True)
            with dve.Fori(1, ETILES // EGRP) as grp:
                group(grp * EGRP)
            evac_y(ETILES - 1, EGRP - 1)
            def combine(t):
                s = t % 4
                dve.wait_ge(gath[s], 32 * (t // 4 + 1))
                if t >= TPB:
                    dve.wait_ge(out_stored[s], 16 * (t // TPB))
                y0, y1, f = gath_sb[0][:, s, :], gath_sb[1][:, s, :], fin[:, s, :]
                steps.did(v.tensor_scalar(y0, y0, pw[:, t, 0:1], None, ALU.mult))
                steps.sync()
                steps.did(v.scalar_tensor_tensor(out=y0, in0=y1, scalar=pw[:, t, 1:2], in1=y0, op0=ALU.mult, op1=ALU.add))
                steps.sync()
                steps.did(v.tensor_tensor(y0, y0, rows[:, t // (NTILE // BATCH), GB, :], ALU.mult))
                steps.sync()
                v.tensor_tensor(f, y0, x_sb[:, t, :], ALU.add).then_inc(comb_done, 1)

            shared_mult(NBLK - 1, between=lambda f: [combine(2 * (f - 1) + k) for k in range(2) if f])
            for t in range(2 * (FTS - 1), NTILE - TPB):
                combine(t)
            shared_add(NBLK - 1)
            for t in range(NTILE - TPB, NTILE):
                combine(t)

        def shared_up(pe, t_, begin, blk):
            if blk == 0:
                pe.wait_ge(ld_sh, 48)
            for f, (f0, m) in enumerate(SH_F):
                for kind, w in (("SA", 0), ("SB", 1)):
                    o = begin((kind, blk, f))
                    for k in range(KC):
                        ins = t_.matmul(o[0:m, :], sup_sb[:, k, w, f0:f0 + m], h2T[:, blk % 2, k, :],
                                        start=(k == 0), stop=(k == KC - 1))
                    ins.then_inc(unit_full, 1)

        def shared_down(pe, t_, begin, blk):
            pe.wait_ge(hs_ready, FTS * (blk + 1))
            for jj in range(2):
                o = begin(("SD", blk, jj))
                for t in range(2):
                    tk = slice((2 * jj + t) * P, (2 * jj + t + 1) * P)
                    for f, (_, m) in enumerate(SH_F):
                        ins = t_.matmul(o[:, t * HID:(t + 1) * HID], hs[0:m, f, tk], sdn_sb[0:m, f, :],
                                        start=(f == 0), stop=(f == FTS - 1))
                ins.then_inc(unit_full, 1)


        @block.tensor
        def _(pe):
            t_ = nc.tensor

            def begin(key):
                n = TURN[key]
                if n >= 2:
                    for s, val in released(UNITS[n - 2]):
                        pe.wait_ge(s, val)
                return bank(key)

            def project(key, w, gr, rhs, rows_=P):
                o = begin(key)
                for k in range(KC):
                    ins = t_.matmul(o[0:rows_, :], w[:, k, gr * P:gr * P + rows_], rhs[:, k, :],
                                    start=(k == 0), stop=(k == KC - 1))
                ins.then_inc(unit_full, 1)

            pe.wait_ge(csil_ready, 1)
            pe.wait_ge(ld_mod, 16)
            o = begin(("MODC", 0, 0))
            for w in range(2):
                for h in range(KC):
                    for k in range(KC):
                        c0 = w * HID + h * P
                        ins = t_.matmul(o[:, (w * KC + h) * BATCH:(w * KC + h + 1) * BATCH], wmod_sb[:, k, c0:c0 + P],
                                        csil[:, k, :], start=(k == 0), stop=(k == KC - 1))
            ins.then_inc(unit_full, 1)
            pe.wait_ge(csilb_ready, 1)
            for b in range(BATCH):
                for h in range(2):
                    o = begin(("MODR", b, h))
                    for k in range(KC):
                        ins = t_.matmul(o[:, :], csil_b[:, k, b, :], wmod_sb[:, k, (h + 1) * 512:(h + 2) * 512],
                                        start=(k == 0), stop=(k == KC - 1))
                    ins.then_inc(unit_full, 1)
            pe.wait_ge(const_pool, 1)

            def inner(b):
                pe.wait_ge(kh_ready, 2 * b + 2)
                pe.wait_ge(qeo_ready, 4 * b + 4)
                for n in (2 * b, 2 * b + 1):
                    for j in range(NPAIR):
                        if n >= 1:
                            pe.wait_ge(atm_ready, NPAIR * (n - 1) + j + 1)
                        r = slice(32 * j, 32 * j + 32)
                        for tl in range(2):
                            for gr in range(KC):
                                for e in range(2):
                                    c = 4 * (n % 2) + 2 * tl + e
                                    q = tl * KC + gr
                                    ins = t_.matmul(at_ps[j][CHUNK * e:CHUNK * (e + 1), q * P:(q + 1) * P],
                                                    kh[r, gr, c * CHUNK:(c + 1) * CHUNK],
                                                    qeo[r, gr, c, :, :].rearrange("p h l -> p (h l)"), start=True, stop=True)
                        ins.then_inc(at_full, 1)
                pe.wait_ge(qf_ready, 2 * b + 2)
                pe.wait_ge(tbd_ready, NPAIR * (b + 1))
                if b >= 1:
                    pe.wait_ge(y_ready, 2 * b)
                for n in (2 * b, 2 * b + 1):
                    pe.wait_ge(atm_ready, NPAIR * (n + 1))
                    for tl in range(2):
                        t = 2 * (n % 2) + tl
                        for gr in range(KC):
                            for e in range(2):
                                c = 2 * t + e
                                reg = slice((gr * TPB + t) * CHUNK, (gr * TPB + t + 1) * CHUNK)
                                inter = c > 0 or b % BPB > 0
                                if inter:
                                    t_.matmul(o_ps[e][:, reg], tbd[:, gr, c, :], qf[:, gr, c * CHUNK:(c + 1) * CHUNK],
                                              start=True, stop=False, skip_group_check=True)
                                ks = slice(CHUNK * e, CHUNK * (e + 1))
                                for h in range(2):
                                    for j in range(NPAIR):
                                        q = (tl * KC + gr) * P + h * CHUNK
                                        ins = t_.matmul(o_ps[e][32 * j:32 * j + 32, reg],
                                                        vpad[ks, t, gr * NPAIR + j, 32 * h:32 * h + 32],
                                                        atm[ks, n % 2, j, q:q + CHUNK],
                                                        start=(not inter and h == 0), stop=(h == 1), skip_group_check=True)
                    ins.then_inc(set_used, 1)

            for s in range(NBLK + 1):
                b = s - 1
                if s < NBLK:
                    pe.wait_ge(xn_ready, s + 1)
                    for k in range(KC):
                        o = begin(("XT", s, k))
                        for t in range(TPB):
                            ins = t_.transpose(o[:, t * P:(t + 1) * P], xn[:, t, k * P:(k + 1) * P], ident[:, :])
                        ins.then_inc(unit_full, 1)
                    if s == 0:
                        pe.wait_ge(ld_wg, 48)
                    pe.wait_ge(ht_ready, 2 * s + 2)
                    project(("LR", s, 0), wg1_sb, 0, hT, LOWR)
                    pe.wait_ge(tt_ready, s + 1)
                    for gr in range(KC):
                        o = begin(("Z", s, gr))
                        t_.matmul(o[:, :], wg2_sb[:, gr * P:(gr + 1) * P], tT[:, :], start=True, stop=True).then_inc(unit_full, 1)
                    if s == 0:
                        pe.wait_ge(ld_wgate, 16)
                    for gr in range(KC):
                        project(("G", s, gr), wgate_sb, gr, hT)
                if s >= 1:
                    inner(b)
                if s < NBLK:
                    if s == 0:
                        pe.wait_ge(ld_wv, 16)
                    for jj in range(2):
                        o = begin(("V", s, jj))
                        for t in range(2):
                            tk = slice((2 * jj + t) * P, (2 * jj + t + 1) * P)
                            for k in range(KC):
                                ins = t_.matmul(o[:, t * HID:(t + 1) * HID], hT[:, k, tk], wv_sb[:, k, :],
                                                start=(k == 0), stop=(k == KC - 1))
                        ins.then_inc(unit_full, 1)
                if s >= 1:
                    for e in range(2):
                        o = begin(("MS", b, e))
                        pe.wait_ge(sq_ready, 2 * b + e + 1)
                        t_.matmul(o[:, :], bd16[:, :], sq[:, e, :], start=True, stop=True).then_inc(unit_full, 1)
                if s < NBLK:
                    if s == 0:
                        pe.wait_ge(ld_wk, 16)
                    for gr in range(KC):
                        project(("K", s, gr), wk_sb, gr, hT)
                if s >= 1:
                    if s == 1:
                        pe.wait_ge(rows_ready, 1)
                    pe.wait_ge(y_ready, 2 * b + 2)
                    for jj in range(2):
                        o = begin(("WO", b, jj))
                        for t in range(2):
                            tk = slice((2 * jj + t) * P, (2 * jj + t + 1) * P)
                            for k in range(KC):
                                ins = t_.matmul(o[:, t * HID:(t + 1) * HID], yT[:, k, tk], wo_sb[:, k, :],
                                                start=(k == 0), stop=(k == KC - 1))
                        ins.then_inc(unit_full, 1)
                if s < NBLK:
                    if s == 0:
                        pe.wait_ge(ld_wq, 16)
                    for gr in range(KC):
                        project(("Q", s, gr), wq_sb, gr, hT)
                    for gr in range(KC):
                        o = begin(("KT", s, gr))
                        pe.wait_ge(kh_ready, 2 * s + gr + 1)
                        for t in range(TPB):
                            ins = t_.transpose(o[:, t * P:(t + 1) * P], kh[:, gr, t * P:(t + 1) * P], ident[:, :])
                        ins.then_inc(unit_full, 1)
                    pe.wait_ge(ktok_ready, 2 * s + 2)
                    pe.wait_ge(v_ready, 2 * s + 2)
                    for e in range(2):
                        o = begin(("KV", s, e))
                        ks = slice(CHUNK * e, CHUNK * (e + 1))
                        for gr in range(KC):
                            for t in range(TPB):
                                reg = slice((gr * TPB + t) * 32, (gr * TPB + t + 1) * 32)
                                for j in range(NPAIR):
                                    r = slice(32 * j, 32 * j + 32)
                                    ins = t_.matmul(o[r, reg], ktok[ks, t, gr, r],
                                                    free_dims(vpad[ks, t, gr * NPAIR + j, 0:1], [[48, 2], [1, HEAD]]),
                                                    start=True, stop=True)
                        ins.then_inc(unit_full, 1)
                if s >= 1:
                    pe.wait_ge(h2tok_ready, s)
                    for k in range(KC):
                        o = begin(("HT", b, k))
                        for t in range(TPB):
                            ins = t_.transpose(o[:, t * P:(t + 1) * P], h2tok[:, b * TPB + t, k * P:(k + 1) * P], ident[:, :])
                        ins.then_inc(unit_full, 1)
                    if s == 1:
                        pe.wait_ge(ld_rout, 16)
                    pe.wait_ge(h2T_ready, 2 * b + 2)
                    o = begin(("RT", b, 0))
                    for t in range(TPB):
                        for k in range(KC):
                            ins = t_.matmul(o[:, t * NROUT:(t + 1) * NROUT], h2T[:, b % 2, k, t * P:(t + 1) * P], rout_sb[:, k, :],
                                            start=(k == 0), stop=(k == KC - 1))
                    ins.then_inc(unit_full, 1)
                for blk in SHARED_AFTER.get(s, ()):
                    shared_up(pe, t_, begin, blk)
                    if blk == RANK_IN:
                        o = begin(("RK", 0, 0))
                        pe.wait_ge(picked_ready, 1)
                        pv = picked[:, :, :].rearrange("p t e -> p (t e)")
                        t_.matmul(o[:, 0:P], tri[:, :], pv, start=True, stop=True)
                        t_.matmul(o[:, P:2 * P], ones[:, :], pv, start=True, stop=True).then_inc(unit_full, 1)
                    shared_down(pe, t_, begin, blk)

            def rows_T(i, u):
                if u % 2 == 0:
                    pe.wait_ge(ld_xt[(u // 2) % 2], 16 * (i // EGRP + 1) if isinstance(i, int) else i0_loads(i, u))
                at_least(pe, xT_ready, i, -1)
                for k in range(KC):
                    ins = t_.transpose(at_ps[u % 2][:, k * P:(k + 1) * P], xt[:, (u // 2) % 2, u % 2, k * P:(k + 1) * P],
                                       ident[:, :])
                ins.then_inc(xt_full, 1)

            def i0_loads(i, u):
                return (i - u) * (16 // EGRP) + 16

            def at_least(eng, s, i, d):
                if not isinstance(i, int) or i + d > 0:
                    eng.wait_ge(s, i + d)

            def up(i, u, e):
                pe.wait_ge(xT_ready, i + 1)
                at_least(pe, h_ready, i, -1)
                for k in range(KC):
                    ins = t_.matmul(at_ps[2 + u % 2][:, 0:2 * FE], xT[:, u % 2, k * P:(k + 1) * P],
                                    eup[:, bass.ds(e, 1), k, :].rearrange("p a n -> p (a n)"), start=(k == 0), stop=(k == KC - 1))
                ins.then_inc(up_full, 1)

            def hid_T(i, u):
                pe.wait_ge(h_ready, i + 1)
                at_least(pe, hTe_ready, i, -1)
                for k in range(2):
                    ins = t_.transpose(o_ps[u % 2][0:FEH, k * P:(k + 1) * P], esil[:, u % 2, k * FEH:(k + 1) * FEH], ident[:, :])
                ins.then_inc(hTp_full, 1)

            def down(i, u, e):
                pe.wait_ge(hTe_ready, i + 1)
                at_least(pe, y_out, i, -1)
                for k in range(2):
                    ins = t_.matmul(work[u % 2][:, 0:HID], hTe[0:FEH, u % 2, k * P:(k + 1) * P],
                                    edn[0:FEH, bass.ds(e, 1), k, :].rearrange("p a n -> p (a n)"), start=(k == 0), stop=(k == 1))
                ins.then_inc(down_full, 1)

            ereg = [pe.alloc_register(f"expert{u}") for u in range(EGRP)]

            def fetch_experts(i0):
                pe.load(ereg, texp_u[0:1, bass.ds(i0, EGRP)])

            def group(i0, before=None, last=False):
                e = [pe.snap(r, min_val=0, max_val=NE - 1) for r in ereg]
                for u in range(EGRP):
                    up(i0 + u, u, e[u])
                    if not (last and u == EGRP - 1):
                        rows_T(i0 + u + 1, (u + 1) % EGRP) if isinstance(i0, int) or u + 1 < EGRP else rows_T_next(i0)
                    if u:
                        down(i0 + u - 1, u - 1, e[u - 1])
                    elif before is not None:
                        down(i0 - 1, EGRP - 1, before)
                    hid_T(i0 + u, u)
                    if u == 0:
                        pe.reg_mov(elast, e[-1])
                        if not last:
                            fetch_experts(i0 + EGRP)

            elast = pe.alloc_register("expert_last")

            def rows_T_next(i0):
                rows_T(i0 + EGRP, 0)

            pe.wait_ge(texp_ready, 1)
            pe.wait_ge(ld_ex, 16 * 2 * NE)
            pe.wait_ge(shev_done, 2 * NBLK - 2)
            fetch_experts(0)
            rows_T(0, 0)
            group(0)
            with pe.Fori(1, ETILES // EGRP - 1) as grp:
                group(grp * EGRP, before=pe.snap(elast, min_val=0, max_val=NE - 1))
            group(ETILES - EGRP, before=pe.snap(elast, min_val=0, max_val=NE - 1), last=True)
            down(ETILES - 1, EGRP - 1, pe.snap(elast, min_val=0, max_val=NE - 1))
            pe.wait_ge(y_out, ETILES)
            shared_up(pe, t_, begin, NBLK - 1)
            shared_down(pe, t_, begin, NBLK - 1)

def kernel(**inputs):
    import numpy as np
    import concourse.bacc as bacc
    from concourse.bass_utils import run_bass_kernel_spmd

    v = {n: np.asarray(a) for n, a in inputs.items()}
    arrays = {
        "x": v["L0_attn_x"].reshape(TOK, HID),
        "cT": v["L0_c"].reshape(BATCH, KC, P).transpose(2, 1, 0),
        "wmod": np.concatenate([v["L0_wmod"][:, i * HID:(i + 1) * HID] for i in (0, 1, 2, 3, 4, 5)], axis=1),
        "wq": v["L0_attn_Wq"], "wk": v["L0_attn_Wk"], "wv": v["L0_attn_Wv"],
        "wg1": v["L0_attn_Wg1"], "wg2": v["L0_attn_Wg2"], "bg2": v["L0_attn_bg2"],
        "wgate": v["L0_attn_Wgate"], "norm_w": v["L0_attn_norm_w"], "wo": v["L0_attn_Wo"],
        "router": np.concatenate([v["L0_ffn_gate_w"], v["L0_ffn_shared_gate_w"]], axis=0).T,
        "e_up": np.concatenate([v["L0_ffn_expert_fc1"], v["L0_ffn_expert_fc2"]], axis=1).transpose(0, 2, 1),
        "e_down": v["L0_ffn_expert_proj"].transpose(0, 2, 1),
        "s_up": np.concatenate([v["L0_ffn_shared_fc1"], v["L0_ffn_shared_fc2"]], axis=0).T,
        "s_down": v["L0_ffn_shared_proj"].T,
    }
    nc = bacc.Bacc("TRN2", target_bir_lowering=False, num_devices=1)
    data, args = {}, {}
    for name, a in arrays.items():
        a = np.ascontiguousarray(a)
        data[f"in_{name}"] = a
        args[name] = nc.dram_tensor(f"in_{name}", a.shape, mybir.dt.from_np(a.dtype), kind="ExternalInput").ap()
    out = nc.dram_tensor("out_rows", (TOK, HID), F32, kind="ExternalOutput").ap()
    adaln_moe(nc, out=out, **args)
    r = run_bass_kernel_spmd(nc, [data], core_ids=[0])
    return r.results[0]["out_rows"].reshape(BATCH, SEQ, HID)
```

```python
from contextlib import ExitStack

import concourse.bass as bass
from concourse import mybir

F32 = mybir.dt.float32
U32 = mybir.dt.uint32
I32 = mybir.dt.int32
ALU = mybir.AluOpType
ACT = mybir.ActivationFunctionType
AX_X = mybir.AxisListType.X

P = 128
BATCH, SEQ, HID = 2, 1024, 256
HEADS, HEAD = 16, 16
CHUNK = 64
LOWR = 16
GATE_NORM = 16.0
EPS = 1e-5
NE, TOPK, FE, FS = 8, 2, 176, 704
TOK = BATCH * SEQ
KC = HID // P
NTILE = TOK // P
BLK = 512
NBLK = TOK // BLK
BPB = SEQ // BLK
TPB = BLK // P
CPB = BLK // CHUNK
NPAIR = P // 32
FEH = FE // 2
FTS = (FS + P - 1) // P
ETILES = 40
EGRP = 4
XS_ROWS = ETILES * P
NROUT = NE + 1
SCALE = HEAD ** -0.5
SH_F = [(f * P, min(P, FS - f * P)) for f in range(FTS)]

def unit_order():
    units = [("MODC", 0, 0)]

    def both(kind, blk):
        units.extend([(kind, blk, 0), (kind, blk, 1)])

    def fill(s, place):
        for part, blk, i in FILL.get((s, place), ()):
            units.extend([("SA", blk, i), ("SB", blk, i)] if part == "U" else [("SD", blk, i)])

    for s in range(NBLK + 1):
        if s < NBLK:
            both("XT", s)
            modr = [("MODR", b, h) for b in range(BATCH) for h in range(2)] if s == 0 else []
            units.extend(modr[0:1])
            fill(s, "turned")
            units.extend([("LR", s, 0)] + modr[1:2])
            fill(s, "low rank")
            both("Z", s)
            units.extend(modr[2:4])
        fill(s, "first")
        if s >= 2:
            both("HT", s - 2)
        if s < NBLK:
            both("G", s)
        if s >= 2:
            units.append(("RT", s - 2, 0))
        fill(s, "gates")
        if s < NBLK:
            units.append(("V", s, 0))
        fill(s, "norm")
        if s < NBLK:
            both("K", s)
            both("Q", s)
            units.append(("V", s, 1))
            both("KT", s)
        if s >= 1:
            both("WO", s - 1)
        if s < NBLK:
            both("KV", s)
    fill(NBLK, "stats")
    fill(NBLK, "ln")
    both("HT", NBLK - 1)
    fill(NBLK, "transposed")
    units.append(("RT", NBLK - 1, 0))
    fill(NBLK, "top2")
    fill(NBLK, "scatter")
    for f in range(FTS):
        units.extend([("SA", NBLK - 1, f), ("SB", NBLK - 1, f)])
    both("SD", NBLK - 1)
    return units


SHARED_PARTS = [(kind, blk, i) for blk in range(NBLK - 1)
                for kind, n in (("U", FTS), ("D", 2)) for i in range(n)]
FILL_PLACES = [(3, "turned", 1), (3, "low rank", 1), (3, "gates", 2), (4, "first", 2), (4, "gates", 1), (4, "norm", 4), (4, "stats", 1), (4, "ln", 1), (4, "transposed", 1), (4, "top2", 1),
               (4, "scatter", len(SHARED_PARTS))]
FILL = {}
for slot_, place_, n_ in FILL_PLACES:
    FILL[slot_, place_] = SHARED_PARTS[:n_]
    del SHARED_PARTS[:n_]
UNITS = unit_order()
TURN = {key: n for n, key in enumerate(UNITS)}


def free_dims(ap, dims):
    return bass.AP(ap.tensor, ap.offset, [list(ap.ap[0])] + [list(d) for d in dims])


def adaln_moe(nc, x, cT, wmod, wq, wk, wv, wg1, wg2, bg2, wgate, norm_w, wo,
              router, e_up, e_down, s_up, s_down, out):
    with ExitStack() as ctx:
        def sb(name, shape, dt=F32):
            return ctx.enter_context(nc.sbuf_tensor(name, shape, dt))

        def ps(name, shape):
            return ctx.enter_context(nc.psum_tensor(name, shape, F32))

        def sem(name):
            return ctx.enter_context(nc.semaphore(name))

        xs_dram = nc.dram_tensor("xs_sorted", (XS_ROWS, HID), F32, kind="Internal").ap()
        ys_dram = nc.dram_tensor("ys_sorted", (XS_ROWS, HID), F32, kind="Internal").ap()

        work = [ps("work0", [P, 512]), ps("work1", [P, 512])]
        at_ps = [ps(f"at_ps{j}", [P, 512]) for j in range(NPAIR)]
        o_ps = [ps("o_even", [P, 512]), ps("o_odd", [P, 512])]

        x_sb = sb("x_sb", [P, NTILE, HID])
        xn = sb("xn", [P, TPB, HID])
        xn2 = sb("xn2", [P, TPB, HID])
        h2tok = sb("h2tok", [P, NTILE, HID])
        h2T = sb("h2T", [P, 2, KC, BLK])
        hT = sb("hT", [P, KC, BLK])
        tT = sb("tT", [33, BLK])
        za = sb("za", [P, KC, BLK])
        h2T_of = [h2T[:, 0, :, :], h2T[:, 1, :, :], za[:, :, :], hT[:, :, :]]
        ktok = za[:, :, :].rearrange("p g (t c) -> p t g c", t=TPB)
        gk = sb("gk", [P, KC, BLK])
        er_pos = sb("er_pos", [P, KC, BLK])
        er_neg = sb("er_neg", [P, KC, BLK])
        arena = sb("arena", [P, 12288])
        taken = [0]

        def part(n):
            taken[0] += n
            assert taken[0] <= 12288
            return arena[:, taken[0] - n:taken[0]]

        qeo = part(KC * BLK * 2).rearrange("p (g c h l) -> p g c h l", g=KC, c=CPB, h=2)
        kh = part(KC * BLK).rearrange("p (g n) -> p g n", g=KC)
        qf = part(KC * BLK).rearrange("p (g n) -> p g n", g=KC)
        vpad = part(TPB * KC * NPAIR * 64).rearrange("p (t r w) -> p t r w", t=TPB, r=KC * NPAIR)
        tbd = part(KC * CPB * P).rearrange("p (g c n) -> p g c n", g=KC, c=CPB)
        atm = part(2 * NPAIR * 512).rearrange("p (a j n) -> p a j n", a=2, j=NPAIR)
        wmod_sb = arena[:, 0:KC * 6 * HID].rearrange("p (k n) -> p k n", k=KC)
        atm_zero = atm[:, 0, 0:2, :].rearrange("p j (t c) -> p (j t) c", c=HID)
        taken[0] = 0
        eup = part(NE * KC * 2 * FE).rearrange("p (e k n) -> p e k n", e=NE, k=KC)
        edn = part(NE * 2 * HID).rearrange("p (e k n) -> p e k n", e=NE, k=2)
        xt = part(2 * 2 * HID).rearrange("p (a t c) -> p a t c", a=2, t=2)
        xT = part(2 * KC * P).rearrange("p (a n) -> p a n", a=2)
        esil = part(2 * FE).rearrange("p (a n) -> p a n", a=2)
        hTe = part(2 * 2 * P).rearrange("p (a n) -> p a n", a=2)
        gbase = sb("gbase", [P, KC, CPB])
        f_base = sb("f_base", [P, KC, CPB])
        f_last = sb("f_last", [P, KC, CPB])
        f_all = sb("f_all", [P, KC, CPB])
        decay = sb("decay", [P, KC, 32, CPB])
        kv_in = sb("kv_in", [P, KC, 32, CPB])
        state = sb("state", [P, 2, KC, 32, CPB])
        carry = sb("carry", [P, KC, 32])
        tmask = sb("tmask", [P, KC, CPB, 32])
        sq = sb("sq", [P, 2, 512])
        yT = sb("yT", [P, KC, BLK])
        sg = sb("sg", [P, 2, KC, BLK])
        tmp = sb("tmp", [P, 2, HID])
        hs = sb("hs", [P, FTS, BLK])

        rows = sb("rows", [P, BATCH, 4, HID])
        GA, SB_, CB1, GB = range(4)
        cols = sb("cols", [P, 2, KC, BATCH])
        csb = sb("csb", [P, KC, BATCH])
        csil = sb("csil", [P, KC, BATCH])

        sgn, mag = (sq[:, b, :].rearrange("p (b c) -> p b c", b=BATCH) for b in range(2))
        csil_b = sg[:, 0, 0, :].rearrange("p (k b n) -> p k b n", k=KC, b=BATCH)
        yflat = yT[:, :, :].rearrange("p k n -> p (k n)")
        onehot = yflat[:, 0:256].rearrange("p (k t e) -> p k t e", k=TOPK, t=NTILE)
        picked, dlog, posf = (yflat[:, i:i + P].rearrange("p (t e) -> p t e", t=NTILE) for i in (256, 384, 512))
        tot, incl, base = (yflat[:, i:i + P].rearrange("p (e t) -> p e t", e=NE) for i in (640, 768, 896))
        tge = sg[:, 1, 0, 0:ETILES * NE].rearrange("p (i e) -> p i e", e=NE)
        pprod = sg[:, 1, 1, 0:P].rearrange("p (t e) -> p t e", t=NTILE)

        wq_sb, wk_sb, wv_sb, wgate_sb, wo_sb = (sb(n, [P, KC, HID]) for n in
                                                ("wq_sb", "wk_sb", "wv_sb", "wgate_sb", "wo_sb"))
        wg1_sb = sb("wg1_sb", [P, KC, LOWR])
        wg2_sb = sb("wg2_sb", [33, HID])
        nw_sb = sb("nw_sb", [P, 1])
        rout_sb = sb("rout_sb", [P, KC, NROUT])
        sup_sb = sb("sup_sb", [P, KC, 2, FS])
        sdn_sb = sb("sdn_sb", [P, FTS, HID])

        ident = sb("ident", [P, P])
        tri = sb("tri", [P, P])
        ones = sb("ones", [P, P])
        bd16 = sb("bd16", [P, P])
        pmask = sb("pmask", [P, 32])
        qsel = sb("qsel", [P, 2])
        causal = sb("causal", [P, 2 * NPAIR, CHUNK])
        eps_c = sb("eps_c", [P, 1])
        iota_i = sb("iota_i", [P, ETILES], I32)
        iota_f = sb("iota_f", [P, ETILES])

        stats = sb("stats", [P, 2, TPB, 6])
        mv = sb("mv", [P, 2, TPB, 2])
        lnv = sb("lnv", [P, 2, TPB])
        rstd = sb("rstd", [P, 2, TPB])
        nmr = sb("nmr", [P, 2, TPB])
        logits = sb("logits", [P, NTILE, NROUT])
        top8 = sb("top8", [P, NTILE, 8])
        top8i = sb("top8i", [P, NTILE, 8], U32)
        topf = sb("topf", [P, TOPK, NTILE])
        sgate_e = sb("sgate_e", [P, NTILE])
        sgate = sb("sgate", [P, NTILE])
        dtop = sb("dtop", [P, NTILE, TOPK])
        psum_p = sb("psum_p", [P, NTILE])
        prec = sb("prec", [P, NTILE])
        pw = sb("pw", [P, NTILE, TOPK])
        resets = sb("resets", [P, BLK])
        rowreset = sb("rowreset", [P, NE, NTILE])
        cnt_i = sb("cnt_i", [P, NE], I32)
        ntl_i = sb("ntl_i", [P, NE], I32)
        ntl = sb("ntl", [P, NE])
        tend = sb("tend", [P, NE])
        tstart = sb("tstart", [P, NE])
        pos = sb("pos", [P, TOPK, NTILE])
        pos_u = sb("pos_u", [P, TOPK, NTILE], U32)
        texp = sb("texp", [P, ETILES])
        texp_u = sb("texp_u", [P, ETILES], U32)

        yout = er_pos[:, :, :].rearrange("p a (t c) -> p a t c", t=2)
        gath_sb = [er_neg[:, :, :].rearrange("p a (t c) -> p (a t) c", t=2),
                   gk[:, :, :].rearrange("p a (t c) -> p (a t) c", t=2)]
        fin = xn

        ld_x = [sem(f"ld_x{i}") for i in range(NBLK)]
        ld_c, ld_mod, ld_wg, ld_wgate, ld_wv, ld_wk, ld_wq, ld_wo, ld_rout, ld_sh, ld_ex = (
            sem(n) for n in ("ld_c", "ld_mod", "ld_wg", "ld_wgate", "ld_wv", "ld_wk", "ld_wq",
                             "ld_wo", "ld_rout", "ld_sh", "ld_ex"))
        xs_zero = sem("xs_zero")
        const_pool, const_dve, zero_ready = sem("const_pool"), sem("const_dve"), sem("zero_ready")
        unit_full = sem("unit_full")
        dve_step, act_step, pool_step = sem("dve_step"), sem("act_step"), sem("pool_step")
        csil_ready, csilb_ready, modc_ready, modr_ready, rows_ready = (
            sem(n) for n in ("csil_ready", "csilb_ready", "modc_ready", "modr_ready", "rows_ready"))
        ln_var, ln_rstd = [sem("ln1_var"), sem("ln2_var")], [sem("ln1_rstd"), sem("ln2_rstd")]
        xn_ready, ht_ready, tt_ready = sem("xn_ready"), sem("ht_ready"), sem("tt_ready")
        zabs_done, zmin_done, zln_done = sem("zabs_done"), sem("zmin_done"), sem("zln_done")
        r_ready, gbase_ready = sem("r_ready"), sem("gbase_ready")
        neg_ready, pos_ready, fac_ready = sem("neg_ready"), sem("pos_ready"), sem("fac_ready")
        sg_ready, v_ready, kh_ready, qeo_ready, qf_ready = (
            sem(n) for n in ("sg_ready", "v_ready", "kh_ready", "qeo_ready", "qf_ready"))
        ktok_ready, kvin_ready, state_ready, decay_ready, tbd_ready = (
            sem(n) for n in ("ktok_ready", "kvin_ready", "state_ready", "decay_ready", "tbd_ready"))
        at_full, atm_ready, set_used = (sem(n) for n in ("at_full", "atm_ready", "set_used"))
        ms_full = sem("ms_full")
        sq_ready, mln_done, rms_ready, m_ready, y_ready = (
            sem(n) for n in ("sq_ready", "mln_done", "rms_ready", "m_ready", "y_ready"))
        woev_done, x1_ready, h2tok_ready, h2T_ready = (
            sem(n) for n in ("woev_done", "x1_ready", "h2tok_ready", "h2T_ready"))
        logit_ready, sge_ready, sgate_ready = sem("logit_ready"), sem("sge_ready"), sem("sgate_ready")
        silu_done, hs_ready, shev_done = sem("silu_done"), sem("hs_ready"), sem("shev_done")
        picked_ready, rank_full, rank_read, dlog_ready, pexp_ready, posu_ready, texp_ready = (
            sem(n) for n in ("picked_ready", "rank_full", "rank_read", "dlog_ready", "pexp_ready", "posu_ready",
                             "texp_ready"))
        xs_ready, ld_xt, xt_full, xT_ready, up_full, esilu_done, h_ready = (
            sem("xs_ready"), [sem("ld_xt0"), sem("ld_xt1")], sem("xt_full"), sem("xT_ready"),
            sem("up_full"), sem("esilu_done"), sem("h_ready"))
        hTp_full, hTe_ready, down_full, y_out, ys_stored = (
            sem("hTp_full"), sem("hTe_ready"), sem("down_full"), sem("y_out"), [sem("ys_st0"), sem("ys_st1")])
        gath = [sem(f"gath{i}") for i in range(4)]
        comb_done, out_stored = sem("comb_done"), [sem(f"out_stored{i}") for i in range(TPB)]

        def released(key):
            kind, blk, j = key
            return {
                "MODC": [(modc_ready, 2)],
                "MODR": [(modr_ready, 2 * blk + j + 1)],
                "XT": [(ht_ready, 2 * blk + j + 1)],
                "LR": [(tt_ready, blk + 1)],
                "Z": [(zabs_done, 2 * blk + j + 1), (zmin_done, 2 * blk + j + 1)],
                "G": [(sg_ready, 2 * blk + j + 1)],
                "V": [(v_ready, 2 * blk + j + 1)],
                "K": [(kh_ready, 2 * blk + j + 1)],
                "WO": [(woev_done, 2 * blk + j + 1)],
                "Q": [(qeo_ready, 4 * blk + 2 * j + 2)],
                "KT": [(ktok_ready, 2 * blk + j + 1)],
                "KV": [(kvin_ready, 2 * blk + j + 1)],
                "HT": [(h2T_ready, 2 * blk + j + 1)],
                "RT": [(logit_ready, blk + 1)],
                "SA": [(silu_done, FTS * blk + j + 1)],
                "SB": [(hs_ready, FTS * blk + j + 1)],
                "SD": [(shev_done, 2 * blk + j + 1)],
            }[kind]

        def bank(key):
            return work[TURN[key] % 2]

        def wait_unit(eng, key):
            eng.wait_ge(unit_full, TURN[key] + 1)

        class Steps:

            def __init__(self, eng, s):
                self.eng, self.s, self.n = eng, s, 0

            def did(self, ins):
                self.n += 1
                ins.then_inc(self.s, 1)
                return self.n

            def sync(self):
                self.eng.wait_ge(self.s, self.n)

        block = ctx.enter_context(nc.Block())

        @block.sync
        def _(sp):
            sp.dma_start(x_sb[:, 0:TPB, :], x[0:BLK, :].rearrange("(t p) c -> p t c", p=P)).then_inc(ld_x[0], 16)
            sp.dma_start(csb[:, :, :], cT).then_inc(ld_c, 16)
            sp.dma_start(wmod_sb, wmod.rearrange("(k p) n -> p k n", p=P)).then_inc(ld_mod, 16)
            sp.dma_start(wg1_sb[:, :, :], wg1.rearrange("(k p) n -> p k n", p=P)).then_inc(ld_wg, 16)
            sp.wait_ge(zero_ready, 3)
            sp.dma_start(wg2_sb[0:LOWR, :], wg2).then_inc(ld_wg, 16)
            sp.dma_start(wg2_sb[32:33, :], bg2.rearrange("(a n) -> a n", a=1)).then_inc(ld_wg, 16)
            for w_sb, w, s in ((wgate_sb, wgate, ld_wgate), (wv_sb, wv, ld_wv), (wk_sb, wk, ld_wk),
                               (wq_sb, wq, ld_wq)):
                sp.dma_start(w_sb[:, :, :], w.rearrange("(k p) n -> p k n", p=P)).then_inc(s, 16)
            for i in range(1, NBLK):
                sp.dma_start(x_sb[:, i * TPB:(i + 1) * TPB, :],
                             x[i * BLK:(i + 1) * BLK, :].rearrange("(t p) c -> p t c", p=P)).then_inc(ld_x[i], 16)
            sp.dma_start(wo_sb[:, :, :], wo.rearrange("(k p) n -> p k n", p=P)).then_inc(ld_wo, 16)
            for h in range(P // HEAD):
                sp.dma_start(nw_sb[h * HEAD:(h + 1) * HEAD, :],
                             norm_w.rearrange("(p a) -> p a", a=1)).then_inc(ld_wo, 16)
            sp.dma_start(rout_sb[:, :, :], router.rearrange("(k p) n -> p k n", p=P)).then_inc(ld_rout, 16)
            sp.dma_start(sup_sb[:, :, :, :].rearrange("p k a f -> p k (a f)"),
                         s_up.rearrange("(k p) n -> p k n", p=P)).then_inc(ld_sh, 16)
            sp.dma_start(sdn_sb[:, 0:FTS - 1, :],
                         s_down[0:(FTS - 1) * P, :].rearrange("(f p) n -> p f n", p=P)).then_inc(ld_sh, 16)
            sp.dma_start(sdn_sb[0:FS - (FTS - 1) * P, FTS - 1, :], s_down[(FTS - 1) * P:FS, :]).then_inc(ld_sh, 16)
            sp.wait_ge(zero_ready, 6)
            for i in range(ETILES // 4):
                sp.dma_start(xs_dram[i * BLK:(i + 1) * BLK, :].rearrange("(t p) c -> p t c", p=P),
                             atm_zero).then_inc(xs_zero, 16)
            sp.wait_ge(set_used, 2 * NBLK)
            for e in range(NE):
                sp.dma_start(eup[:, e, :, :], e_up[e].rearrange("(k p) n -> p k n", p=P)).then_inc(ld_ex, 16)
                sp.dma_start(edn[0:FEH, e, :, :], e_down[e].rearrange("(k p) n -> p k n", p=FEH)).then_inc(ld_ex, 16)
            sp.wait_ge(xs_ready, 16 * TOPK * NTILE)

            def load_pair(q, slot):
                sp.dma_start(xt[:, slot, :, :],
                             xs_dram[bass.ds(q * (2 * P), 2 * P), :].rearrange("(t p) c -> p t c", p=P)
                             ).then_inc(ld_xt[slot], 16)

            def store_pair(q, slot):
                sp.wait_ge(y_out, q * 2 + 2)
                sp.dma_start(ys_dram[bass.ds(q * (2 * P), 2 * P), :].rearrange("(t p) c -> p t c", p=P),
                             yout[:, slot, :, :]).then_inc(ys_stored[slot], 16)

            def load_store(q, slot):
                sp.wait_ge(xt_full, q * 2 - 2)
                load_pair(q, slot)
                store_pair(q - 2, slot)

            load_pair(0, 0)
            load_pair(1, 1)
            with sp.Fori(1, ETILES // EGRP) as grp:
                load_store(grp * 2, 0)
                load_store(grp * 2 + 1, 1)
            for slot in range(2):
                store_pair(ETILES // 2 - 2 + slot, slot)
            for t in range(NTILE):
                sp.wait_ge(comb_done, t + 1)
                sp.dma_start(out[t * P:(t + 1) * P, :], fin[:, t % TPB, :]).then_inc(out_stored[t % TPB], 16)
            for s in out_stored:
                sp.wait_ge(s, 16 * (NTILE // TPB))

        @block.gpsimd
        def _(pool):
            g = nc.gpsimd
            steps = Steps(pool, pool_step)
            steps.did(g.memset(tT[:, :], 0.0))
            g.memset(wg2_sb[:, :], 0.0).then_inc(zero_ready, 1)
            steps.sync()
            pool.wait_ge(zero_ready, 1)
            g.memset(tT[32:33, :], 1.0).then_inc(zero_ready, 1)
            pool.wait_ge(zero_ready, 2)
            g.memset(eps_c[:, :], EPS).then_inc(zero_ready, 1)
            g.memset(vpad, 0.0).then_inc(zero_ready, 1)
            g.memset(tbd, 0.0).then_inc(zero_ready, 1)
            g.memset(atm, 0.0).then_inc(zero_ready, 1)
            steps.did(g.memset(decay[:, :, :, :], 0.0))
            steps.did(g.memset(ident[:, :], 0.0))
            for m in (ones, tri, bd16, causal):
                steps.did(g.memset(m[:, :] if m is not causal else m[:, :, :], 1.0 if m is not bd16 else 1.0 / HEAD))
            steps.did(g.memset(rowreset[:, :, :], 1.0))
            steps.did(g.memset(resets[:, :], 1.0))
            steps.sync()
            steps.did(g.affine_select(out=ident[:, :], in_=ident[:, :], compare_op=ALU.not_equal, fill=1.0,
                                      base=0, pattern=[[-1, P]], channel_multiplier=1))
            steps.did(g.affine_select(out=tri[:, :], in_=tri[:, :], compare_op=ALU.is_gt, fill=0.0,
                                      base=0, pattern=[[1, P]], channel_multiplier=-1))
            bd_v = bd16[:, :].rearrange("p (h v) -> p h v", v=HEAD)
            steps.did(g.affine_select(out=bd_v, in_=bd_v, compare_op=ALU.is_ge, fill=0.0,
                                      base=0, pattern=[[-HEAD, P // HEAD], [0, HEAD]], channel_multiplier=1))
            steps.sync()
            steps.did(g.affine_select(out=bd_v, in_=bd_v, compare_op=ALU.is_ge, fill=0.0,
                                      base=HEAD - 1, pattern=[[HEAD, P // HEAD], [0, HEAD]], channel_multiplier=-1))
            for e in range(2):
                half = causal[CHUNK * e:CHUNK * (e + 1), :, :]
                steps.sync()
                steps.did(g.affine_select(out=half, in_=half, compare_op=ALU.is_ge, fill=0.0,
                                          base=0, pattern=[[0, 2 * NPAIR], [1, CHUNK]], channel_multiplier=-1))
            steps.sync()
            steps.did(g.memset(rowreset[:, :, 0:1], 0.0))
            steps.did(g.memset(resets[:, :].rearrange("p (c l) -> p c l", l=CHUNK)[:, :, 0:1], 0.0))
            steps.did(g.iota(iota_i[:, :], [[1, ETILES]], base=0, channel_multiplier=0))
            steps.sync()
            for j in range(NPAIR):
                q = slice(32 * j, 32 * j + 32)
                steps.did(g.tensor_scalar(pmask[q, :], bd16[q, 32 * j:32 * j + 32], float(HEAD), None, ALU.mult))
                steps.sync()
            g.tensor_scalar(qsel[:, :], pmask[:, :].rearrange("p (h v) -> p h v", v=HEAD)[:, :, 0], SCALE, None,
                            ALU.mult).then_inc(const_pool, 1)

            def tokens_of_chunks(ap, e):
                return ap.rearrange("p g (t h l) -> p g t h l", t=TPB, h=2)[:, :, :, e, :]

            for s in range(NBLK + 1):
                if s >= 1:
                    b = s - 1
                    for e in range(2):
                        pool.wait_ge(rms_ready, 2 * b + e + 1)
                        if e == 0:
                            pool.wait_ge(sg_ready, 2 * b + 2)
                        m = sq[:, e, :].rearrange("p (g t l) -> p g t l", g=KC, t=TPB)
                        g.tensor_tensor(m, m, tokens_of_chunks(sg[:, b % 2, :, :], e), ALU.mult).then_inc(m_ready, 1)
                if s < NBLK:
                    for gr in range(KC):
                        pool.wait_ge(qeo_ready, 4 * s + 2 * gr + 2)
                        g.tensor_tensor(qf[:, gr, :].rearrange("p (c l) -> p c l", c=CPB), qeo[:, gr, :, 0, :],
                                        qeo[:, gr, :, 1, :], ALU.add).then_inc(qf_ready, 1)
                    pool.wait_ge(fac_ready, 2 * s + 2)
                    if s >= 1:
                        pool.wait_ge(state_ready, s)
                    k = steps.did(g.tensor_tensor(f_all[:, :, :], f_base[:, :, :], f_last[:, :, :], ALU.mult))
                    steps.sync()
                    for gr in range(KC):
                        g.tensor_copy(decay[:, gr, :, 1:CPB],
                                      f_all[:, gr, 1:CPB].unsqueeze(1).broadcast_to([P, 32, CPB - 1])).then_inc(decay_ready, 1)
                    steps.did(g.tensor_tensor(
                        tmask[:, :, :, :], f_base[:, :, :].unsqueeze(3).broadcast_to([P, KC, CPB, 32]),
                        free_dims(pmask[:, :], [[0, KC], [0, CPB], [1, 32]]), ALU.mult))
                    steps.sync()
                    pool.wait_ge(state_ready, s + 1)
                    first = 1 if s % BPB == 0 else 0
                    for j in range(NPAIR):
                        q = slice(32 * j, 32 * j + 32)
                        ins = g.tensor_tensor(
                            tbd[q, :, 1:CPB, 32 * j:32 * j + 32],
                            state[q, s % 2, :, :, 0:CPB - 1].rearrange("p g v c -> p g c v"),
                            tmask[q, :, 1:CPB, :], ALU.mult)
                        if not first:
                            steps.did(ins)
                            steps.sync()
                            ins = g.tensor_tensor(tbd[q, :, 0, 32 * j:32 * j + 32], state[q, 1 - s % 2, :, :, CPB - 1],
                                                  tmask[q, :, 0, :], ALU.mult)
                        ins.then_inc(tbd_ready, 1)
                        pool.wait_ge(tbd_ready, NPAIR * s + j + 1)

            pool.wait_ge(xs_zero, 16 * (ETILES // 4))
            pool.wait_ge(posu_ready, 1)
            pool.wait_ge(h2tok_ready, NBLK)
            for k in range(TOPK):
                for t in range(NTILE):
                    g.indirect_dma_start(out=xs_dram, out_offset=bass.IndirectOffsetOnAxis(ap=pos_u[:, k, t:t + 1], axis=0),
                                         in_=h2tok[:, t, :], in_offset=None).then_inc(xs_ready, 16)
            for s in ys_stored:
                pool.wait_ge(s, 16 * (ETILES // 4))
            for t in range(NTILE):
                if t >= 4:
                    pool.wait_ge(comb_done, t - 3)
                for k in range(TOPK):
                    g.indirect_dma_start(out=gath_sb[k][:, t % 4, :], out_offset=None, in_=ys_dram,
                                         in_offset=bass.IndirectOffsetOnAxis(ap=pos_u[:, k, t:t + 1], axis=0)
                                         ).then_inc(gath[t % 4], 16)

        def shared_act(act, a, blk):
            for f in range(FTS):
                silu_up(act, a, blk, f)

        def silu_up(act, a, blk, f):
            m = SH_F[f][1]
            if blk >= 1 and f == 0:
                wait_unit(act, ("SD", blk - 1, 1))
            wait_unit(act, ("SA", blk, f))
            a.activation(hs[0:m, f, :], bank(("SA", blk, f))[0:m, :], ACT.Silu).then_inc(silu_done, 1)

        @block.scalar
        def _(act):
            a = nc.scalar
            steps = Steps(act, act_step)
            act.wait_ge(ld_c, 16)
            a.activation(csil[:, :, :], csb[:, :, :], ACT.Silu).then_inc(csil_ready, 1)
            act.wait_ge(zero_ready, 3)

            def rstd_of(which, n, at):
                act.wait_ge(ln_var[which], n)
                steps.did(a.activation(lnv[:, which, :], mv[:, which, :, 1], ACT.Ln, bias=eps_c[:, 0:1]))
                steps.sync()
                a.activation(rstd[:, which, :], lnv[:, which, :], ACT.Exp, scale=-0.5).then_inc(ln_rstd[which], 1)

            rstd_of(0, 1, 0)

            def evac_mod_rows(b, h):
                wait_unit(act, ("MODR", b, h))
                a.activation(rows[:, b, 2 * h:2 * h + 2, :].rearrange("p a n -> p (a n)"),
                             bank(("MODR", b, h))[:, :], ACT.Copy).then_inc(modr_ready, 1)

            def fill(s, place):
                for kind, blk, f in FILL.get((s, place), ()):
                    if kind == "U":
                        silu_up(act, a, blk, f)

            def evac_h2T(b):
                for k in range(KC):
                    wait_unit(act, ("HT", b, k))
                    a.activation(h2T_of[b][:, k, :], bank(("HT", b, k))[:, :], ACT.Copy).then_inc(h2T_ready, 1)

            def sgate_exp(b):
                act.wait_ge(logit_ready, b + 1)
                a.activation(sgate_e[:, b * TPB:(b + 1) * TPB], logits[:, b * TPB:(b + 1) * TPB, NE], ACT.Exp,
                             scale=-1.0).then_inc(sge_ready, 1)

            def evac_v(s, jj):
                wait_unit(act, ("V", s, jj))
                for t in range(2):
                    ins = a.activation(free_dims(vpad[:, 2 * jj + t, 0, 0:1], [[64, KC * NPAIR], [48, 2], [1, HEAD]]),
                                       bank(("V", s, jj))[:, t * HID:(t + 1) * HID]
                                       .rearrange("p (r h v) -> p r h v", h=2, v=HEAD), ACT.Copy)
                ins.then_inc(v_ready, 1)

            for s in range(NBLK + 1):
                b = s - 1
                if s < NBLK:
                    row = s // BPB
                    if s == 0:
                        act.wait_ge(modc_ready, 2)
                    for k in range(KC):
                        wait_unit(act, ("XT", s, k))
                        a.activation(hT[:, k, :], bank(("XT", s, k))[:, :], ACT.Identity,
                                     bias=cols[:, 0, k, row:row + 1], scale=cols[:, 1, k, row:row + 1]).then_inc(ht_ready, 1)
                    if s == 0:
                        evac_mod_rows(0, 0)
                    fill(s, "turned")
                    wait_unit(act, ("LR", s, 0))
                    a.activation(tT[0:LOWR, :], bank(("LR", s, 0))[0:LOWR, :], ACT.Copy).then_inc(tt_ready, 1)
                    if s == 0:
                        evac_mod_rows(0, 1)
                    fill(s, "low rank")
                    for gr in range(KC):
                        wait_unit(act, ("Z", s, gr))
                        a.activation(za[:, gr, :], bank(("Z", s, gr))[:, :], ACT.Abs).then_inc(zabs_done, 1)
                    if s == 0:
                        evac_mod_rows(1, 0)
                        evac_mod_rows(1, 1)
                fill(s, "first")
                if s >= 2:
                    evac_h2T(s - 2)

                def softplus():
                    act.wait_ge(zabs_done, 2 * s + 2)
                    steps.did(a.activation(za[:, :, :], za[:, :, :], ACT.Exp, scale=-1.0))
                    steps.sync()
                    a.activation(za[:, :, :], za[:, :, :], ACT.Ln, bias=1.0).then_inc(zln_done, 1)

                if s == 0:
                    softplus()
                if s < NBLK:
                    if s >= 2:
                        act.wait_ge(m_ready, 2 * (s - 1))
                    for gr in range(KC):
                        wait_unit(act, ("G", s, gr))
                        a.activation(sg[:, s % 2, gr, :], bank(("G", s, gr))[:, :], ACT.Silu).then_inc(sg_ready, 1)
                fill(s, "gates")
                if 1 <= s < NBLK:
                    softplus()
                if s >= 2:
                    sgate_exp(s - 2)
                if s < NBLK:
                    for gr in range(KC):
                        act.wait_ge(r_ready, 2 * s + gr + 1)
                        if s >= 1 and gr == 0:
                            act.wait_ge(qeo_ready, 4 * s)
                        a.activation(er_neg[:, gr, :], gk[:, gr, :], ACT.Exp, scale=-1.0 / GATE_NORM).then_inc(neg_ready, 1)
                    for gr in range(KC):
                        a.activation(er_pos[:, gr, :], gk[:, gr, :], ACT.Exp, scale=1.0 / GATE_NORM).then_inc(pos_ready, 1)
                    if s >= 1:
                        act.wait_ge(tbd_ready, NPAIR * s)
                        act.wait_ge(state_ready, s)
                    a.activation(f_base[:, :, :], gbase[:, :, :], ACT.Exp, scale=1.0 / GATE_NORM).then_inc(fac_ready, 1)
                    a.activation(f_last[:, :, :], gk[:, :, :].rearrange("p g (c l) -> p g c l", c=CPB)[:, :, :, CHUNK - 1],
                                 ACT.Exp, scale=1.0 / GATE_NORM).then_inc(fac_ready, 1)
                if 1 <= s < NBLK - 1:
                    rstd_of(0, s + 2, 0)
                if s >= 1:
                    act.wait_ge(set_used, 2 * b + 2)
                    for e in range(2):
                        if b >= 1:
                            act.wait_ge(y_ready, 2 * b)
                        else:
                            act.wait_ge(rows_ready, 1)
                        a.activation(sq[:, e, :], o_ps[e][:, :], ACT.Square).then_inc(sq_ready, 1)
                if s == 0:
                    act.wait_ge(zero_ready, 4)
                if s < NBLK:
                    evac_v(s, 0)
                if s >= 1:
                    for e in range(2):
                        act.wait_ge(ms_full, 2 * b + e + 1)
                        a.activation(sq[:, e, :], at_ps[e][:, :], ACT.Ln, bias=eps_c[:, 0:1]).then_inc(mln_done, 1)
                    for e in range(2):
                        act.wait_ge(mln_done, 2 * b + e + 1)
                        a.activation(sq[:, e, :], sq[:, e, :], ACT.Exp, scale=-0.5).then_inc(rms_ready, 1)
                if s < NBLK:
                    evac_v(s, 1)
                fill(s, "norm")
                if s < NBLK:
                    for gr in range(KC):
                        wait_unit(act, ("KT", s, gr))
                        a.activation(ktok[:, :, gr, :], bank(("KT", s, gr))[:, :].rearrange("p (t c) -> p t c", t=TPB),
                                     ACT.Copy).then_inc(ktok_ready, 1)
                if s >= 1:
                    rstd_of(1, s, b)
                if s == 0:
                    rstd_of(0, s + 2, 0)
            fill(NBLK, "stats")
            fill(NBLK, "ln")
            evac_h2T(NBLK - 1)
            fill(NBLK, "transposed")
            sgate_exp(NBLK - 1)
            act.wait_ge(dlog_ready, 2)
            steps.did(a.activation(dlog[:, :, :], dlog[:, :, :], ACT.Exp))
            steps.did(a.activation(pw[:, :, :], dtop[:, :, :], ACT.Exp))
            steps.sync()
            a.activation(dtop[:, :, :], dtop[:, :, :], ACT.Copy).then_inc(pexp_ready, 1)
            fill(NBLK, "top2")
            fill(NBLK, "scatter")

            def evac_rows(i, u):
                act.wait_ge(xt_full, i + 1)
                a.activation(xT[:, u % 2, :], at_ps[u % 2][:, 0:KC * P], ACT.Copy).then_inc(xT_ready, 1)

            def expert_silu(i, u):
                act.wait_ge(up_full, i + 1)
                a.activation(esil[:, u % 2, :], at_ps[2 + u % 2][:, 0:FE], ACT.Silu).then_inc(esilu_done, 1)

            evac_rows(0, 0)

            def group(i0, last=False):
                for u in range(EGRP):
                    expert_silu(i0 + u, u)
                    if not (last and u == EGRP - 1):
                        evac_rows(i0 + u + 1, u + 1)

            with act.Fori(0, ETILES // EGRP - 1) as grp:
                group(grp * EGRP)
            group(ETILES - EGRP, last=True)
            shared_act(act, a, NBLK - 1)

        def routing_a(dve, v, steps):
            dve.wait_ge(const_pool, 1)
            steps.did(v.tensor_copy(iota_f[:, :], iota_i[:, :]))
            steps.did(v.tensor_copy(topf[:, :, :], top8i[:, :, 0:TOPK].rearrange("p t k -> p k t")))
            steps.sync()
            for k in range(TOPK):
                steps.did(v.tensor_tensor(onehot[:, k, :, :], iota_f[:, 0:NE].unsqueeze(1).broadcast_to([P, NTILE, NE]),
                                          topf[:, k, :].unsqueeze(2).broadcast_to([P, NTILE, NE]), ALU.is_equal))
            steps.sync()
            v.tensor_tensor(picked[:, :, :], onehot[:, 0, :, :], onehot[:, 1, :, :], ALU.add).then_inc(picked_ready, 1)
            v.tensor_tensor(dlog[:, :, :], logits[:, :, 0:NE], top8[:, :, 0:1].broadcast_to([P, NTILE, NE]),
                            ALU.subtract).then_inc(dlog_ready, 1)
            v.tensor_tensor(dtop[:, :, :], top8[:, :, 0:TOPK], top8[:, :, 0:1].broadcast_to([P, NTILE, TOPK]),
                            ALU.subtract).then_inc(dlog_ready, 1)

        def routing_b(dve, v, steps):
            dve.wait_ge(rank_full, 1)
            te = at_ps[2][:, P:2 * P].rearrange("p (t e) -> p e t", t=NTILE)
            v.tensor_copy(tot[:, :, :], te).then_inc(rank_read, 1)
            dve.wait_ge(rank_read, 1)
            steps.did(v.tensor_tensor_scan(incl[:, :, :].rearrange("p e t -> p (e t)"),
                                           rowreset[:, :, :].rearrange("p e t -> p (e t)"),
                                           tot[:, :, :].rearrange("p e t -> p (e t)"), 0.0, ALU.mult, ALU.add))
            steps.sync()
            steps.did(v.tensor_scalar(cnt_i[:, :], incl[:, :, NTILE - 1], float(P - 1), None, ALU.add))
            steps.did(v.tensor_tensor(base[:, :, :], incl[:, :, :], tot[:, :, :], ALU.subtract))
            steps.sync()
            steps.did(v.tensor_scalar(ntl_i[:, :], cnt_i[:, :], 7, None, ALU.arith_shift_right))
            steps.sync()
            steps.did(v.tensor_copy(ntl[:, :], ntl_i[:, :]))
            steps.sync()
            steps.did(v.tensor_tensor_scan(tend[:, :], ones[:, 0:NE], ntl[:, :], 0.0, ALU.mult, ALU.add))
            steps.sync()
            steps.did(v.tensor_tensor(tstart[:, :], tend[:, :], ntl[:, :], ALU.subtract))
            steps.did(v.tensor_tensor(tge[:, :, :], iota_f[:, :].unsqueeze(2).broadcast_to([P, ETILES, NE]),
                                      tend[:, :].unsqueeze(1).broadcast_to([P, ETILES, NE]), ALU.is_ge))
            steps.sync()
            steps.did(v.tensor_reduce(texp[:, :], tge[:, :, :], AX_X, ALU.add))
            steps.did(v.tensor_scalar(tstart[:, :], tstart[:, :], float(P), None, ALU.mult))
            steps.sync()
            v.tensor_scalar(texp_u[:, :], texp[:, :], float(NE - 1), None, ALU.min).then_inc(texp_ready, 1)
            steps.did(v.tensor_tensor(base[:, :, :], base[:, :, :], tstart[:, :].unsqueeze(2).broadcast_to([P, NE, NTILE]), ALU.add))
            steps.sync()
            v.tensor_tensor(posf[:, :, :], at_ps[2][:, 0:P].rearrange("p (t e) -> p t e", t=NTILE),
                            base[:, :, :].rearrange("p e t -> p t e"), ALU.add).then_inc(rank_read, 1)
            dve.wait_ge(rank_read, 2)
            for k in range(TOPK):
                steps.did(v.tensor_tensor(pprod[:, :, :], onehot[:, k, :, :], posf[:, :, :], ALU.mult))
                steps.sync()
                steps.did(v.tensor_reduce(pos[:, k, :], pprod[:, :, :], AX_X, ALU.add))
                steps.sync()
            v.tensor_copy(pos_u[:, :, :], pos[:, :, :]).then_inc(posu_ready, 1)
            dve.wait_ge(pexp_ready, 1)
            steps.did(v.tensor_reduce(psum_p[:, :], dlog[:, :, :], AX_X, ALU.add))
            steps.sync()
            steps.did(v.reciprocal(prec[:, :], psum_p[:, :]))
            steps.sync()
            steps.did(v.tensor_tensor(pw[:, :, :], pw[:, :, :], prec[:, :].unsqueeze(2).broadcast_to([P, NTILE, TOPK]), ALU.mult))
            steps.sync()

        @block.vector
        def _(dve):
            v = nc.vector
            steps = Steps(dve, dve_step)

            def ln_stats(which, tile0):
                for t in range(TPB):
                    steps.did(v.bn_stats(stats[:, which, t, :], x_sb[:, tile0 + t, :]))
                steps.sync()
                for t in range(TPB - 1):
                    steps.did(v.bn_aggr(mv[:, which, t, :], stats[:, which, t, :]))
                steps.sync()
                v.bn_aggr(mv[:, which, TPB - 1, :], stats[:, which, TPB - 1, :]).then_inc(ln_var[which], 1)

            def ln_rows(which, n, dst, tile0, last_sem):
                dve.wait_ge(ln_rstd[which], n)
                steps.did(v.scalar_tensor_tensor(out=nmr[:, which, :], in0=mv[:, which, :, 0], scalar=-1.0,
                                                 in1=rstd[:, which, :], op0=ALU.mult, op1=ALU.mult))
                steps.sync()
                for t in range(TPB):
                    ins = v.tensor_scalar(dst[:, t, :], x_sb[:, tile0 + t, :], rstd[:, which, t:t + 1],
                                          nmr[:, which, t:t + 1], ALU.mult, ALU.add)
                    if last_sem is not None and t == TPB - 1:
                        ins.then_inc(last_sem, 1)
                    else:
                        steps.did(ins)

            dve.wait_ge(ld_x[0], 16)
            ln_stats(0, 0)
            dve.wait_ge(csil_ready, 1)
            v.tensor_copy(csil_b[:, :, :, :], csil[:, :, :].unsqueeze(3).broadcast_to([P, KC, BATCH, P])).then_inc(csilb_ready, 1)
            ln_rows(0, 1, xn, 0, xn_ready)
            steps.sync()
            wait_unit(dve, ("MODC", 0, 0))
            modc = bank(("MODC", 0, 0))[:, 0:4 * BATCH].rearrange("p (w k b) -> p w k b", w=2, k=KC)
            v.tensor_copy(cols[:, 0, :, :], modc[:, 0, :, :]).then_inc(modc_ready, 1)
            v.tensor_scalar(cols[:, 1, :, :], modc[:, 1, :, :], 1.0, None, ALU.add).then_inc(modc_ready, 1)
            def finish_mod_rows():
                dve.wait_ge(modr_ready, 4)
                for w in (GA, GB):
                    gv = rows[:, :, w, :]
                    steps.did(v.tensor_scalar(sgn[:, :, :], gv, 0.0, 2.0, ALU.is_ge, ALU.mult))
                    steps.did(v.tensor_scalar(mag[:, :, :], gv, -1.0, None, ALU.mult))
                    steps.sync()
                    steps.did(v.tensor_tensor(mag[:, :, :], mag[:, :, :], gv, ALU.max))
                    steps.sync()
                    steps.did(v.tensor_scalar(mag[:, :, :], mag[:, :, :], 0.25, None, ALU.max))
                    steps.sync()
                    steps.did(v.scalar_tensor_tensor(out=gv, in0=sgn[:, :, :], scalar=-1.0, in1=mag[:, :, :],
                                                     op0=ALU.add, op1=ALU.mult))
                    steps.sync()
                steps.did(v.tensor_scalar(rows[:, :, CB1, :], rows[:, :, CB1, :], 1.0, None, ALU.add))
                dve.wait_ge(ld_wo, 16 * 9)
                for k in range(KC):
                    steps.did(v.tensor_scalar(wo_sb[:, k, :], wo_sb[:, k, :], nw_sb[:, 0:1], None, ALU.mult))
                steps.sync()
                v.engine_nop().then_inc(rows_ready, 1)

            def mult_up(blk, f):
                m = SH_F[f][1]
                dve.wait_ge(silu_done, FTS * blk + f + 1)
                wait_unit(dve, ("SB", blk, f))
                v.tensor_tensor(hs[0:m, f, :], bank(("SB", blk, f))[0:m, :], hs[0:m, f, :], ALU.mult).then_inc(hs_ready, 1)

            def add_down(blk, jj, into=None):
                wait_unit(dve, ("SD", blk, jj))
                steps.sync()
                for t in range(2):
                    tile = blk * TPB + 2 * jj + t
                    ins = v.scalar_tensor_tensor(
                        out=tmp[:, t, :], in0=bank(("SD", blk, jj))[:, t * HID:(t + 1) * HID],
                        scalar=sgate[:, tile:tile + 1], in1=rows[:, blk // BPB, GB, :], op0=ALU.mult, op1=ALU.mult)
                    if t:
                        ins.then_inc(shev_done, 1)
                    else:
                        steps.did(ins)
                dve.wait_ge(shev_done, 2 * blk + jj + 1)
                steps.sync()
                xv = x_sb[:, blk * TPB + 2 * jj:blk * TPB + 2 * jj + 2, :]
                if into is None:
                    steps.did(v.tensor_tensor(xv, xv, tmp[:, :, :], ALU.add))
                else:
                    v.tensor_tensor(into, xv, tmp[:, :, :], ALU.add).then_inc(comb_done, 2)

            def fill(s, place):
                for kind, blk, i in FILL.get((s, place), ()):
                    (mult_up if kind == "U" else add_down)(blk, i)

            def evac_logits(b):
                tl = slice(b * TPB, (b + 1) * TPB)
                wait_unit(dve, ("RT", b, 0))
                v.tensor_copy(logits[:, tl, :], bank(("RT", b, 0))[:, 0:TPB * NROUT].rearrange("p (t e) -> p t e", t=TPB)
                              ).then_inc(logit_ready, 1)

            def top_two(b):
                tl = slice(b * TPB, (b + 1) * TPB)
                dve.wait_ge(logit_ready, b + 1)
                for t in range(b * TPB, (b + 1) * TPB):
                    steps.did(v.max(top8[:, t, :], logits[:, t, 0:NE]))
                steps.sync()
                for t in range(b * TPB, (b + 1) * TPB):
                    steps.did(v.max_index(top8i[:, t, :], top8[:, t, :], logits[:, t, 0:NE]))
                dve.wait_ge(sge_ready, b + 1)
                steps.did(v.tensor_scalar(sgate[:, tl], sgate_e[:, tl], 1.0, None, ALU.add))
                steps.sync()
                steps.did(v.reciprocal(sgate[:, tl], sgate[:, tl]))
                steps.sync()

            def ln1_of(blk):
                dve.wait_ge(ld_x[blk], 16)
                ln_stats(0, blk * TPB)
                wait_unit(dve, ("XT", blk - 1, 1))
                ln_rows(0, blk + 1, xn, blk * TPB, xn_ready)

            dve.wait_ge(const_pool, 1)
            for s in range(NBLK + 1):
                b = s - 1
                if s < NBLK:
                    fill(s, "turned")
                    fill(s, "low rank")
                    if s >= 1:
                        dve.wait_ge(pos_ready, 2 * s)
                        dve.wait_ge(fac_ready, 2 * s)
                    for gr in range(KC):
                        wait_unit(dve, ("Z", s, gr))
                        if gr == 0:
                            dve.wait_ge(zabs_done, 2 * s + 1)
                        else:
                            dve.wait_ge(zabs_done, 2 * s + 2)
                        v.tensor_scalar(gk[:, gr, :], bank(("Z", s, gr))[:, :], 0.0, None, ALU.min).then_inc(zmin_done, 1)

                def log_gates():
                    dve.wait_ge(zln_done, s + 1)
                    for gr in range(KC):
                        dve.wait_ge(zmin_done, 2 * s + gr + 1)
                        steps.did(v.tensor_tensor(gk[:, gr, :], gk[:, gr, :], za[:, gr, :], ALU.subtract))
                        steps.sync()
                        starts = gk[:, gr, :].rearrange("p (c l) -> p c l", c=CPB)[:, :, 0]
                        v.tensor_copy(gbase[:, gr, :], starts).then_inc(gbase_ready, 1)
                        dve.wait_ge(gbase_ready, 2 * s + gr + 1)
                        steps.did(v.memset(starts, 0.0))
                        steps.sync()
                        v.tensor_tensor_scan(gk[:, gr, :], resets[:, :], gk[:, gr, :], 0.0,
                                             ALU.mult, ALU.add).then_inc(r_ready, 1)

                if s == 0:
                    log_gates()
                fill(s, "first")
                if s >= 2:
                    evac_logits(s - 2)
                fill(s, "gates")
                if s >= 1:
                    if s == 1:
                        dve.wait_ge(xs_zero, 16 * (ETILES // 4))
                        dve.wait_ge(zero_ready, 6)
                    for n in (2 * b, 2 * b + 1):
                        if n >= 2:
                            dve.wait_ge(set_used, n - 1)
                        for j in range(NPAIR):
                            dve.wait_ge(at_full, NPAIR * n + j + 1)
                            v.copy_predicated(atm[:, n % 2, j, :], causal[:, :, :].bitcast(U32).rearrange("p r l -> p (r l)"),
                                              at_ps[j][:, :]).then_inc(atm_ready, 1)
                if 1 <= s < NBLK:
                    log_gates()
                if s >= 2:
                    top_two(s - 2)
                if 1 <= s < NBLK - 1:
                    ln1_of(s + 1)
                if s < NBLK:
                    for gr in range(KC):
                        wait_unit(dve, ("K", s, gr))
                        dve.wait_ge(neg_ready, 2 * s + gr + 1)
                        v.tensor_tensor(kh[:, gr, :], bank(("K", s, gr))[:, :], er_neg[:, gr, :], ALU.mult).then_inc(kh_ready, 1)
                if s < NBLK:
                    for gr in range(KC):
                        wait_unit(dve, ("Q", s, gr))
                        dve.wait_ge(pos_ready, 2 * s + gr + 1)
                        for h in range(2):
                            v.scalar_tensor_tensor(
                                out=qeo[:, gr, :, h, :], in0=bank(("Q", s, gr))[:, :].rearrange("p (c l) -> p c l", c=CPB),
                                scalar=qsel[:, h:h + 1], in1=er_pos[:, gr, :].rearrange("p (c l) -> p c l", c=CPB),
                                op0=ALU.mult, op1=ALU.mult).then_inc(qeo_ready, 1)
                fill(s, "norm")
                if s == 0:
                    ln1_of(1)
                if s >= 1:
                    for e in range(2):
                        dve.wait_ge(m_ready, 2 * b + e + 1)
                        ov = o_ps[e][:, :].rearrange("p (g t l) -> p g t l", g=KC, t=TPB)
                        yv = yT[:, :, :].rearrange("p g (t h l) -> p g t h l", t=TPB, h=2)[:, :, :, e, :]
                        v.tensor_tensor(yv, ov, sq[:, e, :].rearrange("p (g t l) -> p g t l", g=KC, t=TPB),
                                        ALU.mult).then_inc(y_ready, 1)
                    for jj in range(2):
                        wait_unit(dve, ("WO", b, jj))
                        steps.sync()
                        ga2 = rows[:, b // BPB, GA, :].unsqueeze(1).broadcast_to([P, 2, HID])
                        v.tensor_tensor(tmp[:, :, :], bank(("WO", b, jj))[:, :].rearrange("p (t c) -> p t c", t=2), ga2,
                                        ALU.mult).then_inc(woev_done, 1)
                        dve.wait_ge(woev_done, 2 * b + jj + 1)
                        xv = x_sb[:, b * TPB + 2 * jj:b * TPB + 2 * jj + 2, :]
                        steps.did(v.tensor_tensor(xv, xv, tmp[:, :, :], ALU.add))
                if s >= 1:
                    steps.sync()
                    ln_stats(1, b * TPB)
                if s < NBLK:
                    dve.wait_ge(fac_ready, 2 * s + 2)
                    if s >= 1:
                        steps.sync()
                    kv_v = kv_in[:, :, :, :].rearrange("p g v (t h) -> p g t h v", h=2)
                    for e in range(2):
                        wait_unit(dve, ("KV", s, e))
                        fl = f_last[:, :, :].rearrange("p g (t h) -> p g t h", h=2)[:, :, :, e]
                        v.tensor_tensor(kv_v[:, :, :, e, :], bank(("KV", s, e))[:, 0:256].rearrange("p (g t v) -> p g t v", g=KC, t=TPB),
                                        fl.unsqueeze(3).broadcast_to([P, KC, TPB, 32]), ALU.mult).then_inc(kvin_ready, 1)
                    dve.wait_ge(kvin_ready, 2 * s + 2)
                    dve.wait_ge(decay_ready, 2 * s + 2)
                    if s % BPB:
                        steps.did(v.tensor_tensor(carry[:, :, :], state[:, 1 - s % 2, :, :, CPB - 1],
                                                  f_all[:, :, 0:1].broadcast_to([P, KC, 32]), ALU.mult))
                        steps.sync()
                        steps.did(v.tensor_tensor(kv_in[:, :, :, 0], kv_in[:, :, :, 0], carry[:, :, :], ALU.add))
                        steps.sync()
                    if s >= 1:
                        dve.wait_ge(tbd_ready, NPAIR * s)
                    v.tensor_tensor_scan(state[:, s % 2, :, :, :].rearrange("p g v c -> p (g v c)"),
                                         decay[:, :, :, :].rearrange("p g v c -> p (g v c)"),
                                         kv_in[:, :, :, :].rearrange("p g v c -> p (g v c)"), 0.0,
                                         ALU.mult, ALU.add).then_inc(state_ready, 1)
                if s == NBLK:
                    fill(s, "stats")
                if s >= 1:
                    ln_rows(1, s, xn2, b * TPB, None)
                    steps.sync()
                    ht = h2tok[:, b * TPB:(b + 1) * TPB, :]
                    bc = [rows[:, b // BPB, w, :].unsqueeze(1).broadcast_to([P, TPB, HID]) for w in (CB1, SB_)]
                    steps.did(v.tensor_tensor(xn2[:, :, :], xn2[:, :, :], bc[0], ALU.mult))
                    steps.sync()
                    v.tensor_tensor(ht, xn2[:, :, :], bc[1], ALU.add).then_inc(h2tok_ready, 1)
                if s == 0:
                    finish_mod_rows()
            fill(NBLK, "ln")
            fill(NBLK, "transposed")
            evac_logits(NBLK - 1)
            top_two(NBLK - 1)
            routing_a(dve, v, steps)
            routing_b(dve, v, steps)
            fill(NBLK, "top2")
            fill(NBLK, "scatter")

            def expert_h(i, u):
                dve.wait_ge(esilu_done, i + 1)
                v.tensor_tensor(esil[:, u % 2, :], at_ps[2 + u % 2][:, FE:2 * FE], esil[:, u % 2, :],
                                ALU.mult).then_inc(h_ready, 1)

            def evac_hT(i, u):
                dve.wait_ge(hTp_full, i + 1)
                v.tensor_copy(hTe[0:FEH, u % 2, :], o_ps[u % 2][0:FEH, 0:2 * P]).then_inc(hTe_ready, 1)

            def evac_y(i, u):
                dve.wait_ge(down_full, i + 1)
                v.tensor_copy(yout[:, (u // 2) % 2, u % 2, :], work[u % 2][:, 0:HID]).then_inc(y_out, 1)

            def group(i0, first=False):
                for u in range(EGRP):
                    expert_h(i0 + u, u)
                    if not (first and u == 0):
                        if not first and u in (1, 3):
                            slot = 0 if u == 1 else 1
                            dve.wait_ge(ys_stored[slot], stored_before(i0, slot))
                        evac_y(i0 + u - 1, (u - 1) % EGRP)
                    evac_hT(i0 + u, u)

            def stored_before(i0, slot):
                return 16 * (i0 // EGRP) if isinstance(i0, int) else i0 * (16 // EGRP)

            group(0, first=True)
            with dve.Fori(1, ETILES // EGRP) as grp:
                group(grp * EGRP)
            evac_y(ETILES - 1, EGRP - 1)
            def combine(t):
                s = t % 4
                last = t >= NTILE - TPB
                dve.wait_ge(gath[s], 32 * (t // 4 + 1))
                if t >= TPB and not last:
                    dve.wait_ge(out_stored[s], 16 * (t // TPB))
                y0, y1, f = gath_sb[0][:, s, :], gath_sb[1][:, s, :], fin[:, s, :]
                steps.did(v.tensor_scalar(y0, y0, pw[:, t, 0:1], None, ALU.mult))
                steps.sync()
                steps.did(v.scalar_tensor_tensor(out=y0, in0=y1, scalar=pw[:, t, 1:2], in1=y0, op0=ALU.mult, op1=ALU.add))
                steps.sync()
                steps.did(v.tensor_tensor(y0, y0, rows[:, t // (NTILE // BATCH), GB, :], ALU.mult))
                steps.sync()
                if last:
                    steps.did(v.tensor_tensor(x_sb[:, t, :], y0, x_sb[:, t, :], ALU.add))
                else:
                    v.tensor_tensor(f, y0, x_sb[:, t, :], ALU.add).then_inc(comb_done, 1)

            for f in range(FTS):
                if f:
                    combine(2 * f - 2)
                    combine(2 * f - 1)
                mult_up(NBLK - 1, f)
            for t in range(2 * (FTS - 1), NTILE - TPB + 2):
                combine(t)
            for jj in range(2):
                if jj:
                    combine(NTILE - 2)
                    combine(NTILE - 1)
                for i in range(2 * jj, 2 * jj + 2):
                    dve.wait_ge(out_stored[i], 16 * (NTILE // TPB - 1))
                add_down(NBLK - 1, jj, into=fin[:, 2 * jj:2 * jj + 2, :])

        def shared_up(pe, t_, begin, blk, f):
            if blk == 0 and f == 0:
                pe.wait_ge(ld_sh, 48)
            f0, m = SH_F[f]
            for kind, w in (("SA", 0), ("SB", 1)):
                o = begin((kind, blk, f))
                for k in range(KC):
                    ins = t_.matmul(o[0:m, :], sup_sb[:, k, w, f0:f0 + m], h2T_of[blk][:, k, :],
                                    start=(k == 0), stop=(k == KC - 1))
                ins.then_inc(unit_full, 1)

        def shared_down(pe, t_, begin, blk, jj):
            pe.wait_ge(hs_ready, FTS * (blk + 1))
            o = begin(("SD", blk, jj))
            for t in range(2):
                tk = slice((2 * jj + t) * P, (2 * jj + t + 1) * P)
                for f, (_, m) in enumerate(SH_F):
                    ins = t_.matmul(o[:, t * HID:(t + 1) * HID], hs[0:m, f, tk], sdn_sb[0:m, f, :],
                                    start=(f == 0), stop=(f == FTS - 1))
            ins.then_inc(unit_full, 1)

        @block.tensor
        def _(pe):
            t_ = nc.tensor

            def begin(key):
                n = TURN[key]
                if n >= 2:
                    for s, val in released(UNITS[n - 2]):
                        pe.wait_ge(s, val)
                return bank(key)

            def project(key, w, gr, rhs, rows_=P):
                o = begin(key)
                for k in range(KC):
                    ins = t_.matmul(o[0:rows_, :], w[:, k, gr * P:gr * P + rows_], rhs[:, k, :],
                                    start=(k == 0), stop=(k == KC - 1))
                ins.then_inc(unit_full, 1)

            pe.wait_ge(csil_ready, 1)
            pe.wait_ge(ld_mod, 16)
            o = begin(("MODC", 0, 0))
            for w in range(2):
                for h in range(KC):
                    for k in range(KC):
                        c0 = w * HID + h * P
                        ins = t_.matmul(o[:, (w * KC + h) * BATCH:(w * KC + h + 1) * BATCH], wmod_sb[:, k, c0:c0 + P],
                                        csil[:, k, :], start=(k == 0), stop=(k == KC - 1))
            ins.then_inc(unit_full, 1)
            pe.wait_ge(csilb_ready, 1)

            def mod_rows(b, h):
                o = begin(("MODR", b, h))
                for k in range(KC):
                    ins = t_.matmul(o[:, :], csil_b[:, k, b, :], wmod_sb[:, k, (h + 1) * 512:(h + 2) * 512],
                                    start=(k == 0), stop=(k == KC - 1))
                ins.then_inc(unit_full, 1)

            pe.wait_ge(const_pool, 1)

            def inner(b):
                pe.wait_ge(kh_ready, 2 * b + 2)
                pe.wait_ge(qeo_ready, 4 * b + 4)
                if b >= 1:
                    pe.wait_ge(mln_done, 2 * b)
                for n in (2 * b, 2 * b + 1):
                    for j in range(NPAIR):
                        if n >= 1:
                            pe.wait_ge(atm_ready, NPAIR * (n - 1) + j + 1)
                        r = slice(32 * j, 32 * j + 32)
                        for tl in range(2):
                            for gr in range(KC):
                                for e in range(2):
                                    c = 4 * (n % 2) + 2 * tl + e
                                    q = tl * KC + gr
                                    ins = t_.matmul(at_ps[j][CHUNK * e:CHUNK * (e + 1), q * P:(q + 1) * P],
                                                    kh[r, gr, c * CHUNK:(c + 1) * CHUNK],
                                                    qeo[r, gr, c, :, :].rearrange("p h l -> p (h l)"), start=True, stop=True)
                        ins.then_inc(at_full, 1)
                pe.wait_ge(qf_ready, 2 * b + 2)
                pe.wait_ge(tbd_ready, NPAIR * (b + 1))
                if b >= 1:
                    pe.wait_ge(y_ready, 2 * b)
                for n in (2 * b, 2 * b + 1):
                    pe.wait_ge(atm_ready, NPAIR * (n + 1))
                    for tl in range(2):
                        t = 2 * (n % 2) + tl
                        for gr in range(KC):
                            for e in range(2):
                                c = 2 * t + e
                                reg = slice((gr * TPB + t) * CHUNK, (gr * TPB + t + 1) * CHUNK)
                                inter = c > 0 or b % BPB > 0
                                if inter:
                                    t_.matmul(o_ps[e][:, reg], tbd[:, gr, c, :], qf[:, gr, c * CHUNK:(c + 1) * CHUNK],
                                              start=True, stop=False, skip_group_check=True)
                                ks = slice(CHUNK * e, CHUNK * (e + 1))
                                for h in range(2):
                                    for j in range(NPAIR):
                                        q = (tl * KC + gr) * P + h * CHUNK
                                        ins = t_.matmul(o_ps[e][32 * j:32 * j + 32, reg],
                                                        vpad[ks, t, gr * NPAIR + j, 32 * h:32 * h + 32],
                                                        atm[ks, n % 2, j, q:q + CHUNK],
                                                        start=(not inter and h == 0), stop=(h == 1), skip_group_check=True)
                    ins.then_inc(set_used, 1)

            def fill(s, place):
                for kind, blk, i in FILL.get((s, place), ()):
                    (shared_up if kind == "U" else shared_down)(pe, t_, begin, blk, i)

            def transpose_h2(b):
                pe.wait_ge(h2tok_ready, b + 1)
                for k in range(KC):
                    o = begin(("HT", b, k))
                    for t in range(TPB):
                        ins = t_.transpose(o[:, t * P:(t + 1) * P], h2tok[:, b * TPB + t, k * P:(k + 1) * P], ident[:, :])
                    ins.then_inc(unit_full, 1)

            def router(b):
                pe.wait_ge(h2T_ready, 2 * b + 2)
                o = begin(("RT", b, 0))
                for t in range(TPB):
                    for k in range(KC):
                        ins = t_.matmul(o[:, t * NROUT:(t + 1) * NROUT], h2T_of[b][:, k, t * P:(t + 1) * P], rout_sb[:, k, :],
                                        start=(k == 0), stop=(k == KC - 1))
                ins.then_inc(unit_full, 1)

            def values(s, jj):
                o = begin(("V", s, jj))
                for t in range(2):
                    tk = slice((2 * jj + t) * P, (2 * jj + t + 1) * P)
                    for k in range(KC):
                        ins = t_.matmul(o[:, t * HID:(t + 1) * HID], hT[:, k, tk], wv_sb[:, k, :],
                                        start=(k == 0), stop=(k == KC - 1))
                ins.then_inc(unit_full, 1)

            for s in range(NBLK + 1):
                b = s - 1
                if s < NBLK:
                    pe.wait_ge(xn_ready, s + 1)
                    for k in range(KC):
                        o = begin(("XT", s, k))
                        for t in range(TPB):
                            ins = t_.transpose(o[:, t * P:(t + 1) * P], xn[:, t, k * P:(k + 1) * P], ident[:, :])
                        ins.then_inc(unit_full, 1)
                    if s == 0:
                        mod_rows(0, 0)
                        pe.wait_ge(ld_wg, 48)
                    fill(s, "turned")
                    pe.wait_ge(ht_ready, 2 * s + 2)
                    project(("LR", s, 0), wg1_sb, 0, hT, LOWR)
                    if s == 0:
                        mod_rows(0, 1)
                    fill(s, "low rank")
                    pe.wait_ge(tt_ready, s + 1)
                    for gr in range(KC):
                        o = begin(("Z", s, gr))
                        t_.matmul(o[:, :], wg2_sb[:, gr * P:(gr + 1) * P], tT[:, :], start=True, stop=True).then_inc(unit_full, 1)
                    if s == 0:
                        mod_rows(1, 0)
                        mod_rows(1, 1)
                fill(s, "first")
                if s >= 2:
                    transpose_h2(s - 2)
                if s < NBLK:
                    if s == 0:
                        pe.wait_ge(ld_wgate, 16)
                    for gr in range(KC):
                        project(("G", s, gr), wgate_sb, gr, hT)
                if s >= 2:
                    if s == 2:
                        pe.wait_ge(ld_rout, 16)
                    router(s - 2)
                fill(s, "gates")
                if s >= 1:
                    inner(b)
                if s < NBLK:
                    if s == 0:
                        pe.wait_ge(ld_wv, 16)
                    values(s, 0)
                if s >= 1:
                    for e in range(2):
                        pe.wait_ge(sq_ready, 2 * b + e + 1)
                        t_.matmul(at_ps[e][:, :], bd16[:, :], sq[:, e, :], start=True, stop=True).then_inc(ms_full, 1)
                fill(s, "norm")
                if s < NBLK:
                    if s == 0:
                        pe.wait_ge(ld_wk, 16)
                    for gr in range(KC):
                        project(("K", s, gr), wk_sb, gr, hT)
                    if s == 0:
                        pe.wait_ge(ld_wq, 16)
                    for gr in range(KC):
                        project(("Q", s, gr), wq_sb, gr, hT)
                    values(s, 1)
                    for gr in range(KC):
                        o = begin(("KT", s, gr))
                        pe.wait_ge(kh_ready, 2 * s + gr + 1)
                        for t in range(TPB):
                            ins = t_.transpose(o[:, t * P:(t + 1) * P], kh[:, gr, t * P:(t + 1) * P], ident[:, :])
                        ins.then_inc(unit_full, 1)
                if s >= 1:
                    if s == 1:
                        pe.wait_ge(rows_ready, 1)
                    pe.wait_ge(y_ready, 2 * b + 2)
                    for jj in range(2):
                        o = begin(("WO", b, jj))
                        for t in range(2):
                            tk = slice((2 * jj + t) * P, (2 * jj + t + 1) * P)
                            for k in range(KC):
                                ins = t_.matmul(o[:, t * HID:(t + 1) * HID], yT[:, k, tk], wo_sb[:, k, :],
                                                start=(k == 0), stop=(k == KC - 1))
                        ins.then_inc(unit_full, 1)
                if s < NBLK:
                    pe.wait_ge(ktok_ready, 2 * s + 2)
                    pe.wait_ge(v_ready, 2 * s + 2)
                    for e in range(2):
                        o = begin(("KV", s, e))
                        ks = slice(CHUNK * e, CHUNK * (e + 1))
                        for gr in range(KC):
                            for t in range(TPB):
                                reg = slice((gr * TPB + t) * 32, (gr * TPB + t + 1) * 32)
                                for j in range(NPAIR):
                                    r = slice(32 * j, 32 * j + 32)
                                    ins = t_.matmul(o[r, reg], ktok[ks, t, gr, r],
                                                    free_dims(vpad[ks, t, gr * NPAIR + j, 0:1], [[48, 2], [1, HEAD]]),
                                                    start=True, stop=True)
                        ins.then_inc(unit_full, 1)
            fill(NBLK, "stats")
            fill(NBLK, "ln")
            transpose_h2(NBLK - 1)
            fill(NBLK, "transposed")
            router(NBLK - 1)
            fill(NBLK, "top2")
            pe.wait_ge(picked_ready, 1)
            pv = picked[:, :, :].rearrange("p t e -> p (t e)")
            t_.matmul(at_ps[2][:, 0:P], tri[:, :], pv, start=True, stop=True)
            t_.matmul(at_ps[2][:, P:2 * P], ones[:, :], pv, start=True, stop=True).then_inc(rank_full, 1)
            fill(NBLK, "scatter")

            def rows_T(i, u):
                if u % 2 == 0:
                    pe.wait_ge(ld_xt[(u // 2) % 2], 16 * (i // EGRP + 1) if isinstance(i, int) else i0_loads(i, u))
                at_least(pe, xT_ready, i, -1)
                for k in range(KC):
                    ins = t_.transpose(at_ps[u % 2][:, k * P:(k + 1) * P], xt[:, (u // 2) % 2, u % 2, k * P:(k + 1) * P],
                                       ident[:, :])
                ins.then_inc(xt_full, 1)

            def i0_loads(i, u):
                return (i - u) * (16 // EGRP) + 16

            def at_least(eng, s, i, d):
                if not isinstance(i, int) or i + d > 0:
                    eng.wait_ge(s, i + d)

            def up(i, u, e):
                pe.wait_ge(xT_ready, i + 1)
                at_least(pe, h_ready, i, -1)
                for k in range(KC):
                    ins = t_.matmul(at_ps[2 + u % 2][:, 0:2 * FE], xT[:, u % 2, k * P:(k + 1) * P],
                                    eup[:, bass.ds(e, 1), k, :].rearrange("p a n -> p (a n)"), start=(k == 0), stop=(k == KC - 1))
                ins.then_inc(up_full, 1)

            def hid_T(i, u):
                pe.wait_ge(h_ready, i + 1)
                at_least(pe, hTe_ready, i, -1)
                for k in range(2):
                    ins = t_.transpose(o_ps[u % 2][0:FEH, k * P:(k + 1) * P], esil[:, u % 2, k * FEH:(k + 1) * FEH], ident[:, :])
                ins.then_inc(hTp_full, 1)

            def down(i, u, e):
                pe.wait_ge(hTe_ready, i + 1)
                at_least(pe, y_out, i, -1)
                for k in range(2):
                    ins = t_.matmul(work[u % 2][:, 0:HID], hTe[0:FEH, u % 2, k * P:(k + 1) * P],
                                    edn[0:FEH, bass.ds(e, 1), k, :].rearrange("p a n -> p (a n)"), start=(k == 0), stop=(k == 1))
                ins.then_inc(down_full, 1)

            ereg = [pe.alloc_register(f"expert{u}") for u in range(EGRP)]

            def fetch_experts(i0):
                pe.load(ereg, texp_u[0:1, bass.ds(i0, EGRP)])

            def group(i0, before=None, last=False):
                e = [pe.snap(r, min_val=0, max_val=NE - 1) for r in ereg]
                for u in range(EGRP):
                    up(i0 + u, u, e[u])
                    if not (last and u == EGRP - 1):
                        rows_T(i0 + u + 1, (u + 1) % EGRP) if isinstance(i0, int) or u + 1 < EGRP else rows_T_next(i0)
                    if u:
                        down(i0 + u - 1, u - 1, e[u - 1])
                    elif before is not None:
                        down(i0 - 1, EGRP - 1, before)
                    hid_T(i0 + u, u)
                    if u == 0:
                        pe.reg_mov(elast, e[-1])
                        if not last:
                            fetch_experts(i0 + EGRP)

            elast = pe.alloc_register("expert_last")

            def rows_T_next(i0):
                rows_T(i0 + EGRP, 0)

            pe.wait_ge(texp_ready, 1)
            pe.wait_ge(ld_ex, 16 * 2 * NE)
            pe.wait_ge(shev_done, 2 * NBLK - 2)
            pe.wait_ge(mln_done, 2 * NBLK)
            pe.wait_ge(rank_read, 2)
            fetch_experts(0)
            rows_T(0, 0)
            group(0)
            with pe.Fori(1, ETILES // EGRP - 1) as grp:
                group(grp * EGRP, before=pe.snap(elast, min_val=0, max_val=NE - 1))
            group(ETILES - EGRP, before=pe.snap(elast, min_val=0, max_val=NE - 1), last=True)
            down(ETILES - 1, EGRP - 1, pe.snap(elast, min_val=0, max_val=NE - 1))
            pe.wait_ge(y_out, ETILES)
            for f in range(FTS):
                shared_up(pe, t_, begin, NBLK - 1, f)
            for jj in range(2):
                shared_down(pe, t_, begin, NBLK - 1, jj)

def kernel(**inputs):
    import numpy as np
    import concourse.bacc as bacc
    from concourse.bass_utils import run_bass_kernel_spmd

    v = {n: np.asarray(a) for n, a in inputs.items()}
    arrays = {
        "x": v["L0_attn_x"].reshape(TOK, HID),
        "cT": v["L0_c"].reshape(BATCH, KC, P).transpose(2, 1, 0),
        "wmod": np.concatenate([v["L0_wmod"][:, i * HID:(i + 1) * HID] for i in (0, 1, 2, 3, 4, 5)], axis=1),
        "wq": v["L0_attn_Wq"], "wk": v["L0_attn_Wk"], "wv": v["L0_attn_Wv"],
        "wg1": v["L0_attn_Wg1"], "wg2": v["L0_attn_Wg2"], "bg2": v["L0_attn_bg2"],
        "wgate": v["L0_attn_Wgate"], "norm_w": v["L0_attn_norm_w"], "wo": v["L0_attn_Wo"],
        "router": np.concatenate([v["L0_ffn_gate_w"], v["L0_ffn_shared_gate_w"]], axis=0).T,
        "e_up": np.concatenate([v["L0_ffn_expert_fc1"], v["L0_ffn_expert_fc2"]], axis=1).transpose(0, 2, 1),
        "e_down": v["L0_ffn_expert_proj"].transpose(0, 2, 1),
        "s_up": np.concatenate([v["L0_ffn_shared_fc1"], v["L0_ffn_shared_fc2"]], axis=0).T,
        "s_down": v["L0_ffn_shared_proj"].T,
    }
    nc = bacc.Bacc("TRN2", target_bir_lowering=False, num_devices=1)
    data, args = {}, {}
    for name, a in arrays.items():
        a = np.ascontiguousarray(a)
        data[f"in_{name}"] = a
        args[name] = nc.dram_tensor(f"in_{name}", a.shape, mybir.dt.from_np(a.dtype), kind="ExternalInput").ap()
    out = nc.dram_tensor("out_rows", (TOK, HID), F32, kind="ExternalOutput").ap()
    adaln_moe(nc, out=out, **args)
    r = run_bass_kernel_spmd(nc, [data], core_ids=[0])
    return r.results[0]["out_rows"].reshape(BATCH, SEQ, HID)
```
